# Optimizing a Trainium2 kernel written in Bass

```python
import numpy as np
import jax
import jax.numpy as jnp

def _softmax(x, axis=-1):
    return jax.nn.softmax(x, axis=axis)

def _gelu(x):
    return jax.nn.gelu(x, approximate=True)

def _silu(x):
    return jax.nn.silu(x)

def _sigmoid(x):
    return jax.nn.sigmoid(x)

def _layernorm(x, axis=-1, eps=1e-05):
    m = jnp.mean(x, axis=axis, keepdims=True)
    v = jnp.var(x, axis=axis, keepdims=True)
    return (x - m) / jnp.sqrt(v + eps)

def _scatter_add(tgt, idx, src, axis=0):
    return tgt.at[idx].add(src)

def _segment_sum(src, seg, n):
    return jax.ops.segment_sum(src, seg, n)
kernel_name = 'mk_gnn_resnorm_d1_gnn_r8_119b18'

def setup_inputs(seed: int=0):
    np.random.seed(seed)
    _w = jnp.asarray

    def _rec_inputs():
        import jax
        import jax.numpy as jnp
        _gk = jax.random.key(seed)
        x = -0.0003713 + 1 * jax.random.normal(jax.random.fold_in(_gk, 1), (12500, 128), jnp.float32)
        _s = jax.random.randint(jax.random.fold_in(_gk, 2), (100000,), 0, 12500, jnp.int32)
        _d = jax.random.randint(jax.random.fold_in(_gk, 3), (100000,), 0, 12500, jnp.int32)
        _loop = jnp.arange(12500, dtype=jnp.int32)
        src = jnp.concatenate([_s, _d, _loop])
        dst = jnp.concatenate([_d, _s, _loop])
        _o = jnp.argsort(dst, stable=True)
        src = src[_o]
        dst = dst[_o]
        edge_type_8 = jax.random.randint(jax.random.fold_in(_gk, 12), (212500,), 0, 8, jnp.int32)
        return (x, src, dst, edge_type_8)
    x, src, dst, edge_type_8 = _rec_inputs()

    def _L0_gnn_setup():
        import jax, jax.numpy as jnp
        import numpy as np
        N_NODES = 12500
        N_EDGES = 75000
        HID = 128
        N_ETYPES = 8
        key = jax.random.key(seed)
        ks = jax.random.split(key, 10)
        s = 1.0 / np.sqrt(HID)
        return {'h': jax.random.normal(ks[0], (N_NODES, HID), dtype=jnp.float32), 'edge_index': jax.random.randint(ks[1], (2, N_EDGES), 0, N_NODES, dtype=jnp.int64), 'edge_type': jax.random.randint(ks[2], (N_EDGES,), 0, N_ETYPES, dtype=jnp.int64), 'message_W': jax.random.uniform(ks[3], (N_ETYPES, HID, HID), jnp.float32, -s, s), 'message_b': jax.random.uniform(ks[4], (N_ETYPES, HID), jnp.float32, -s, s), 'gru_w_ih': jax.random.uniform(ks[5], (3 * HID, HID), jnp.float32, -s, s), 'gru_w_hh': jax.random.uniform(ks[6], (3 * HID, HID), jnp.float32, -s, s), 'gru_b_ih': jax.random.uniform(ks[7], (3 * HID,), jnp.float32, -s, s), 'gru_b_hh': jax.random.uniform(ks[8], (3 * HID,), jnp.float32, -s, s)}
    _L0_gnn_all = _L0_gnn_setup()
    _L0_gnn_in = {k: v for k, v in _L0_gnn_all.items() if k in ('message_W', 'message_b', 'gru_w_ih', 'gru_w_hh', 'gru_b_ih', 'gru_b_hh')}
    del _L0_gnn_all
    return {'x': x, 'src': src, 'dst': dst, 'edge_type_8': edge_type_8, 'L0_gnn_message_W': _L0_gnn_in['message_W'], 'L0_gnn_message_b': _L0_gnn_in['message_b'], 'L0_gnn_gru_w_ih': _L0_gnn_in['gru_w_ih'], 'L0_gnn_gru_w_hh': _L0_gnn_in['gru_w_hh'], 'L0_gnn_gru_b_ih': _L0_gnn_in['gru_b_ih'], 'L0_gnn_gru_b_hh': _L0_gnn_in['gru_b_hh']}

def reference(x, src, dst, edge_type_8, L0_gnn_message_W, L0_gnn_message_b, L0_gnn_gru_w_ih, L0_gnn_gru_w_hh, L0_gnn_gru_b_ih, L0_gnn_gru_b_hh):
    import jax
    import jax.numpy as jnp

    def _L0_gnn_ref(h, edge_index, edge_type, message_W, message_b, gru_w_ih, gru_w_hh, gru_b_ih, gru_b_hh):
        import jax, jax.numpy as jnp
        import numpy as np
        N_NODES = 12500
        N_EDGES = 75000
        HID = 128
        N_ETYPES = 8
        num_nodes = h.shape[0]
        src, dst = (edge_index[0], edge_index[1])
        all_msgs = jnp.einsum('nh,thd->ntd', h, message_W) + message_b
        msg = all_msgs[src, edge_type]
        messages = jax.ops.segment_sum(msg, dst, num_segments=num_nodes)
        gi = messages @ gru_w_ih.T + gru_b_ih
        gh = h @ gru_w_hh.T + gru_b_hh
        i_r, i_z, i_n = jnp.split(gi, 3, axis=-1)
        h_r, h_z, h_n = jnp.split(gh, 3, axis=-1)
        r = jax.nn.sigmoid(i_r + h_r)
        z = jax.nn.sigmoid(i_z + h_z)
        n = jnp.tanh(i_n + r * h_n)
        return (1.0 - z) * n + z * h
    edge_index = jnp.stack([src, dst])
    x = _layernorm(x + _L0_gnn_ref(x, edge_index, edge_type_8, L0_gnn_message_W, L0_gnn_message_b, L0_gnn_gru_w_ih, L0_gnn_gru_w_hh, L0_gnn_gru_b_ih, L0_gnn_gru_b_hh), axis=-1)
    return x

_drawn_inputs = setup_inputs


def setup_inputs(seed=0):
    import zlib

    import numpy as np

    out = dict(_drawn_inputs(seed))
    spreads = {}
    factors = {'L0_gnn_gru_b_ih': 4.308, 'L0_gnn_gru_b_hh': 5.666}
    for name, (base, spread) in spreads.items():
        noise = np.random.default_rng([zlib.crc32(name.encode()), seed]).standard_normal(out[name].shape)
        drawn = base * np.exp(spread * noise) if base else spread * noise
        out[name] = jnp.asarray(drawn.astype(out[name].dtype))
    for name, factor in factors.items():
        out[name] = (out[name] * factor).astype(out[name].dtype)
    return out
```

```python
from contextlib import ExitStack

import concourse.bass as bass
from concourse import mybir

P = 128
F32 = mybir.dt.float32
BF16 = mybir.dt.bfloat16
I32 = mybir.dt.int32
ALU = mybir.AluOpType
ACT = mybir.ActivationFunctionType
AX = mybir.AxisListType.X
EPS = 1e-5
NEWTON = 3


def gnn_kernel(nc, x, src, dst, etype, w_msg, b_msg, w_ih, w_hh, b_ih, b_hh, out):
    ds = bass.ds
    NODES, HID = x.shape
    EDGES = src.shape[0]
    TYPES = w_msg.shape[0]
    TILES = -(-EDGES // P)
    NODE_TILES = -(-NODES // P)
    ROUND = -(-TILES // NODE_TILES)
    GROUPS = (6, 6, 5)
    START = (0, 6, 12)
    SPAN = 16
    WINDOW = 64
    LAG = 2
    LAST = TILES - (NODE_TILES - 1) * ROUND
    LAST_GROUPS = 2
    assert sum(GROUPS) == ROUND and LAST == GROUPS[0] + GROUPS[1] and HID == P
    BLOCKS = -(-TILES // P)
    FULL = EDGES // P - (BLOCKS - 1) * P
    REST = EDGES % P
    COLS = BLOCKS * P
    PAD_ROW = NODES + P
    ACC_ROWS = (NODE_TILES + 1) * P
    NODE_LAST = NODES - (NODE_TILES - 1) * P
    GATE = 3 * HID
    assert PAD_ROW < ACC_ROWS and NODES - 1 + WINDOW <= ACC_ROWS

    acc = nc.dram_tensor("message_rows", (ACC_ROWS, HID), F32, kind="Internal").ap()

    ctx = ExitStack()
    with ctx:
        def sb(name, shape, dt=F32):
            return ctx.enter_context(nc.sbuf_tensor(name, shape, dt))

        def pb(name):
            return ctx.enter_context(nc.psum_tensor(name, [P, 512], F32))

        def sem(name):
            return ctx.enter_context(nc.semaphore(name))

        dst_rows = sb("dst_rows", [P, BLOCKS, P], I32)
        src_rows = sb("src_rows", [P, BLOCKS, P], I32)
        type_rows = sb("type_rows", [P, BLOCKS, P], I32)
        src_f = sb("src_f", [P, BLOCKS, P])
        type_f = sb("type_f", [P, BLOCKS, P])
        rel_f = sb("rel_f", [P, BLOCKS, P])
        rel_real = sb("rel_real", [P, BLOCKS, P])
        src_T = sb("src_T", [P, COLS])
        type_T = sb("type_T", [P, COLS])
        rel_T = sb("rel_T", [P, COLS])
        ROW = NODE_TILES * ROUND
        first_dst = sb("first_dst", [1, ROW], I32)
        offset = sb("offset", [1, ROW], I32)
        rising = sb("rising", [1, ROW])
        bound = sb("bound", [1, NODE_TILES], I32)
        ahead = sb("ahead", [1, NODE_TILES])
        checks = sb("checks", [1, 8])
        bad = sb("bad", [P, 4])
        fits = sb("fits", [1, 1], I32)
        ident = sb("ident", [P, P])
        ones = sb("ones", [P, P])
        row0 = sb("row0", [P, P])
        earlier = sb("earlier", [P, P])
        zeros = sb("zeros", [P, 512], BF16)
        iota_i = sb("iota_i", [P, SPAN], I32)
        iota_f = sb("iota_f", [P, SPAN])
        spare_i = sb("spare_i", [P, 1], I32)
        spare_f = sb("spare_f", [P, 1])
        w_type = sb("w_type", [P, TYPES, HID])
        b_type = sb("b_type", [P, HID])
        b_wide = sb("b_wide", [P, TYPES * HID])
        w_ih_rows = sb("w_ih_rows", [P, 3, HID])
        w_hh_rows = sb("w_hh_rows", [P, 3, HID])
        w_ih_T = sb("w_ih_T", [P, GATE])
        w_hh_T = sb("w_hh_T", [P, GATE])
        bi_row = sb("bi_row", [1, GATE])
        bh_row = sb("bh_row", [1, GATE])
        gate_bias = sb("gate_bias", [P, 512])
        idx = sb("idx", [P, ROUND], I32)
        rows = sb("rows", [P, ROUND, HID])
        node_mask = [sb(f"node_mask{c}", [P, n, SPAN], BF16) for c, n in enumerate(GROUPS)]
        type_mask = [sb(f"type_mask{c}", [P, n, P], BF16) for c, n in enumerate(GROUPS)]
        onehot = [sb(f"onehot{c}", [P, n, SPAN, TYPES]) for c, n in enumerate(GROUPS)]
        sums = [sb(f"sums{c}", [P, TYPES, WINDOW]) for c in range(3)]
        counts = [sb(f"counts{c}", [P, WINDOW]) for c in range(3)]
        messages_T = sb("messages_T", [P, ACC_ROWS])
        x_tile = sb("x_tile", [P, HID])
        x_T = sb("x_T", [P, P])
        messages = sb("messages", [P, P])
        rz = sb("rz", [P, 2 * HID])
        t_rh = sb("t_rh", [P, HID])
        t_pre = sb("t_pre", [P, HID])
        t_n = sb("t_n", [P, HID])
        t_d = sb("t_d", [P, HID])
        t_zd = sb("t_zd", [P, HID])
        t_h = sb("t_h", [P, HID])
        t_y = sb("t_y", [P, HID])
        stats = sb("stats", [P, nc.vector.BN_STATS_DIM])
        mean_var = sb("mean_var", [P, nc.vector.BN_AGGR_DIM])
        var_eps = sb("var_eps", [P, 1])
        half_bits = sb("half_bits", [P, 1], I32)
        root_a = sb("root_a", [P, 1])
        root_b = sb("root_b", [P, 1])
        rstd = sb("rstd", [P, 1])
        out_tile = sb("out_tile", [P, HID])
        g_dst_T = sb("g_dst_T", [P, COLS])
        g_idx = sb("g_idx", [P, 1], I32)
        g_col = sb("g_col", [P, 1])
        g_wide = sb("g_wide", [P, P])
        g_types = sb("g_types", [P, TYPES])
        g_rows = sb("g_rows", [P, HID])
        g_rows_T = sb("g_rows_T", [P, P])
        g_same = sb("g_same", [P, P])
        g_before = sb("g_before", [P, P])
        g_n = sb("g_n", [P, 1])
        g_first = sb("g_first", [P, 1])
        g_rise = sb("g_rise", [P, 1])
        g_row = sb("g_row", [P, 1], I32)
        g_msg = sb("g_msg", [P, HID])
        g_sum = sb("g_sum", [P, HID])
        g_acc = sb("g_acc", [P, HID])

        agg = [pb(f"agg{c}") for c in range(3)]
        cnt = [pb(f"cnt{c}") for c in range(2)]
        msg = pb("msg")
        gates = pb("gates")
        xt = pb("xt")

        filled = sem("filled")
        dst_in = sem("dst_in")
        first_in = sem("first_in")
        src_in = sem("src_in")
        type_in = sem("type_in")
        weights_in = sem("weights_in")
        consts = sem("consts")
        zeroed = sem("zeroed")
        prep = sem("prep")
        rel_ready = sem("rel_ready")
        src_f_ready = sem("src_f_ready")
        type_f_ready = sem("type_f_ready")
        turned = sem("turned")
        turned_copied = sem("turned_copied")
        bad_ready = sem("bad_ready")
        bad_summed = sem("bad_summed")
        fits_ready = sem("fits_ready")
        gathered = [sem(f"gathered{k}") for k in range(ROUND)]
        idx_ready = [sem(f"idx_ready{c}") for c in range(3)]
        node_mask_ready = [sem(f"node_mask_ready{c}") for c in range(3)]
        type_mask_ready = [sem(f"type_mask_ready{c}") for c in range(3)]
        onehot_ready = [sem(f"onehot_ready{c}") for c in range(3)]
        tiles_done = [sem(f"tiles_done{c}") for c in range(3)]
        sums_copied = [sem(f"sums_copied{c}") for c in range(3)]
        applied = [sem(f"applied{c}") for c in range(3)]
        added = [sem(f"added{c}") for c in range(3)]
        x_in = sem("x_in")
        xt_ready = sem("xt_ready")
        xt_copied = sem("xt_copied")
        messages_copied = sem("messages_copied")
        gates_ready = sem("gates_ready")
        rz_ready = sem("rz_ready")
        rh_ready = sem("rh_ready")
        pre_ready = sem("pre_ready")
        n_ready = sem("n_ready")
        d_ready = sem("d_ready")
        zd_ready = sem("zd_ready")
        h_ready = sem("h_ready")
        y_ready = sem("y_ready")
        stats_ready = sem("stats_ready")
        mv_ready = sem("mv_ready")
        root_step = [sem(f"root_step{n}") for n in range(3 + 3 * NEWTON)]
        out_ready = sem("out_ready")
        out_stored = sem("out_stored")
        g_dst_f = sem("g_dst_f")
        g_turned = sem("g_turned")
        g_turned_copied = sem("g_turned_copied")
        g_idx_ready = sem("g_idx_ready")
        g_col_ready = sem("g_col_ready")
        g_wide_ready = sem("g_wide_ready")
        g_gathered = sem("g_gathered")
        g_xt_ready = sem("g_xt_ready")
        g_xt_copied = sem("g_xt_copied")
        g_prod_ready = sem("g_prod_ready")
        g_step = sem("g_step")
        g_msg_ready = sem("g_msg_ready")
        g_sum_ready = sem("g_sum_ready")
        g_sum_copied = sem("g_sum_copied")
        g_added = sem("g_added")
        g_acc_in = sem("g_acc_in")
        g_acc_turned = sem("g_acc_turned")
        g_acc_copied = sem("g_acc_copied")

        block = ctx.enter_context(nc.Block())

        TURNS = [(a, b0, min(4, BLOCKS - b0)) for a in range(3) for b0 in range(0, BLOCKS, 4)]
        N_FILLED = 4
        N_CONSTS = 6
        N_ZEROED = 5
        PREP_GATE = 3

        def load_flag(engine):
            engine.wait_ge(fits_ready, 1)
            return nc.values_load(fits[0:1, 0:1], engines=[engine.engine], min_val=0, max_val=1,
                                  skip_runtime_bounds_check_because="it is a product of comparisons")

        def groups_of(last):
            return range(LAST_GROUPS if last else 3)

        def each_round(engine, body):
            for r in range(LAG + 1):
                body(r, r == LAG, False)
            with engine.Fori(LAG + 1, NODE_TILES - 2) as r:
                body(r, True, False)
            body(NODE_TILES - 2, True, False)
            body(NODE_TILES - 1, True, True)

        def each_node_tile(engine, body):
            body(0)
            with engine.Fori(1, NODE_TILES) as j:
                body(j)

        def wait_used(engine, semaphore, count):
            if not (isinstance(count, int) and count == 0):
                engine.wait_ge(semaphore, count)

        @block.sync
        def _(sp):
            def load_rows(tile, values, done):
                whole = (BLOCKS - 1) * P * P
                sp.dma_start(tile[:, 0:BLOCKS - 1, :],
                             values[0:whole].rearrange("(b p e) -> p b e", p=P, e=P)).then_inc(done, 16)
                sp.dma_start(tile[0:FULL, BLOCKS - 1, :],
                             values[whole:whole + FULL * P].rearrange("(p e) -> p e", e=P)).then_inc(done, 16)
                sp.dma_start(tile[FULL:FULL + 1, BLOCKS - 1, 0:REST],
                             values[EDGES - REST:EDGES].rearrange("(p e) -> p e", p=1)).then_inc(done, 16)

            sp.wait_ge(filled, N_FILLED)
            with nc.allow_non_contiguous_dma(reason="the first dst of every edge tile, once"):
                sp.dma_start(first_dst[0:1, 0:TILES],
                             dst[0:EDGES:P].rearrange("(p e) -> p e", p=1)).then_inc(first_in, 16)
            load_rows(dst_rows, dst, dst_in)
            load_rows(src_rows, src, src_in)
            load_rows(type_rows, etype, type_in)

            def load_x(j, n=P):
                sp.dma_start(x_tile[0:n, :], x[ds(j * P, n), :]).then_inc(x_in, 16)

            def store_out(j, n=P):
                sp.wait_ge(out_ready, j + 1)
                sp.dma_start(out[ds(j * P, n), :], out_tile[0:n, :]).then_inc(out_stored, 16)

            def node_tiles():
                load_x(0)
                with sp.Fori(0, NODE_TILES - 2) as j:
                    store_out(j)
                    load_x(j + 1)
                store_out(NODE_TILES - 2)
                load_x(NODE_TILES - 1, NODE_LAST)
                store_out(NODE_TILES - 1, NODE_LAST)
                sp.wait_ge(out_stored, 16 * NODE_TILES)

            flag = load_flag(sp)
            with sp.If(flag):
                node_tiles()
            with sp.Else():
                sp.wait_ge(g_added, 16 * (TILES + 1))
                def load_acc(j):
                    wait_used(sp, g_acc_copied, j)
                    sp.dma_start(g_acc[:, :], acc[ds(j * P, P), :]).then_inc(g_acc_in, 16)

                each_node_tile(sp, load_acc)
                node_tiles()

        @block.gpsimd
        def _(pool):
            nc.gpsimd.memset(ident[:], 0.0).then_inc(consts, 1)
            nc.gpsimd.memset(ones[:], 1.0).then_inc(consts, 1)
            nc.gpsimd.iota(iota_i[:], pattern=[[1, SPAN]], base=0, channel_multiplier=0).then_inc(consts, 1)
            nc.gpsimd.iota(bound[:], pattern=[[P, NODE_TILES]], base=-P * (LAG - 1),
                           channel_multiplier=0).then_inc(consts, 1)
            nc.gpsimd.iota(spare_i[:], pattern=[[0, 1]], base=NODES, channel_multiplier=1).then_inc(consts, 1)
            pool.wait_ge(consts, 5)
            nc.gpsimd.affine_select(out=ident[:], in_=ident[:], compare_op=ALU.not_equal, fill=1.0, base=0,
                                    pattern=[[-1, P]], channel_multiplier=1)
            nc.gpsimd.affine_select(out=earlier[:], in_=ones[:], compare_op=ALU.is_gt, fill=0.0, base=0,
                                    pattern=[[-1, P]], channel_multiplier=1).then_inc(consts, 1)

            def gather_round(due, last=False):
                for c in groups_of(last):
                    pool.wait_ge(fits_ready, 1)
                    pool.wait_ge(idx_ready[c], due)
                    for k in range(START[c], START[c] + GROUPS[c]):
                        nc.gpsimd.indirect_dma_start(
                            out=rows[:, k, :], out_offset=None, in_=x[:, :],
                            in_offset=bass.IndirectOffsetOnAxis(ap=idx[:, k:k + 1], axis=0),
                        ).then_inc(gathered[k], 16)

            flag = load_flag(pool)
            with pool.If(flag):
                with pool.Fori(1, NODE_TILES) as due:
                    gather_round(due)
                gather_round(NODE_TILES, last=True)
            with pool.Else():
                pool.wait_ge(zeroed, N_ZEROED)
                nc.gpsimd.dma_start(acc.rearrange("(p r) d -> p (r d)", p=P), messages_T[:, :]).then_inc(g_added, 16)
                pool.wait_ge(g_added, 16)
                with pool.Fori(1, TILES + 1) as due:
                    pool.wait_ge(fits_ready, 1)
                    pool.wait_ge(g_idx_ready, due)
                    nc.gpsimd.indirect_dma_start(
                        out=g_rows[:, :], out_offset=None, in_=x[:, :],
                        in_offset=bass.IndirectOffsetOnAxis(ap=g_idx[:, 0:1], axis=0),
                    ).then_inc(g_gathered, 16)
                    pool.wait_ge(fits_ready, 1)
                    pool.wait_ge(g_sum_copied, due)
                    nc.gpsimd.indirect_dma_start(
                        out=acc[:, :], out_offset=bass.IndirectOffsetOnAxis(ap=g_row[:, 0:1], axis=0),
                        in_=g_sum[:, :], in_offset=None, compute_op=ALU.add,
                    ).then_inc(g_added, 16)
                    pool.wait_ge(g_added, (due + 1) * 16)

        @block.scalar
        def _(act):
            act.wait_ge(zeroed, N_ZEROED)
            act.dma_start(w_type[:, :, :], w_msg.rearrange("t h d -> h t d")).then_inc(weights_in, 16)
            act.dma_start(b_type[0:TYPES, :], b_msg).then_inc(weights_in, 16)
            act.dma_start(b_wide[0:1, :], b_msg.rearrange("(o t) d -> o (t d)", o=1)).then_inc(weights_in, 16)
            act.dma_start(w_ih_rows[:, :, :], w_ih.rearrange("(a p) h -> p a h", p=P)).then_inc(weights_in, 16)
            act.dma_start(w_hh_rows[:, :, :], w_hh.rearrange("(a p) h -> p a h", p=P)).then_inc(weights_in, 16)
            act.dma_start(bi_row[0:1, :], b_ih.rearrange("(o n) -> o n", o=1)).then_inc(weights_in, 16)
            act.dma_start(bh_row[0:1, :], b_hh.rearrange("(o n) -> o n", o=1)).then_inc(weights_in, 16)

            act.wait_ge(src_in, 48)
            nc.scalar.activation(src_f[:, :, :], src_rows[:, :, :], ACT.Copy).then_inc(src_f_ready, 1)
            act.wait_ge(type_in, 48)
            nc.scalar.activation(type_f[:, :, :], type_rows[:, :, :], ACT.Copy).then_inc(type_f_ready, 1)
            for n, (a, b0, nb) in enumerate(TURNS):
                act.wait_ge(turned, n + 1)
                nc.scalar.activation((src_T, rel_T, type_T)[a][:, b0 * P:(b0 + nb) * P],
                                     agg[n % 3][:, 0:nb * P], ACT.Copy).then_inc(turned_copied, 1)
            act.wait_ge(turned, len(TURNS) + 2)
            nc.scalar.activation(w_ih_T[:, :], gates[:, 0:GATE], ACT.Copy).then_inc(turned_copied, 1)
            nc.scalar.activation(w_hh_T[:, :], msg[:, 0:GATE], ACT.Copy).then_inc(turned_copied, 1)

            def next_indices(r, c):
                a = r * ROUND + START[c]
                nc.scalar.activation(idx[:, START[c]:START[c] + GROUPS[c]], src_T[:, ds(a, GROUPS[c])],
                                     ACT.Copy).then_inc(idx_ready[c], 1)

            def copy_sums(r, c, more):
                act.wait_ge(tiles_done[c], r + 1)
                wait_used(act, applied[c], r)
                nc.scalar.activation(sums[c][:, :, :],
                                     agg[c][:, :].rearrange("p (n t) -> p t n", t=TYPES), ACT.Copy)
                nc.scalar.activation(counts[c][:, :], cnt[c % 2][:, 0:WINDOW], ACT.Copy).then_inc(sums_copied[c], 1)
                if more:
                    next_indices(r + 1, c)

            def finish(j, nodes_added):
                act.wait_ge(xt_ready, j + 1)
                wait_used(act, gates_ready, j)
                nc.scalar.activation(x_T[:, :], xt[:, 0:P], ACT.Copy).then_inc(xt_copied, 1)
                act.wait_ge(*nodes_added)
                nc.scalar.activation(messages[:, :], messages_T[:, ds(j * P, P)], ACT.Copy).then_inc(messages_copied, 1)
                act.wait_ge(gates_ready, j + 1)
                wait_used(act, out_ready, j)
                nc.scalar.activation(rz[:, :], gates[:, 0:2 * HID], ACT.Sigmoid).then_inc(rz_ready, 1)
                act.wait_ge(pre_ready, j + 1)
                nc.scalar.activation(t_n[:, :], t_pre[:, :], ACT.Tanh).then_inc(n_ready, 1)

            def round_(r, fin, last):
                more = (lambda c: not last) if not isinstance(r, int) else (lambda c: r + 1 < NODE_TILES - 1 or (not last and c < LAST_GROUPS))
                copy_sums(r, 0, more(0))
                if fin:
                    finish(r - LAG, (added[2], r))
                copy_sums(r, 1, more(1))
                if not last:
                    copy_sums(r, 2, more(2))

            flag = load_flag(act)
            with act.If(flag):
                act.wait_ge(turned_copied, 4)
                for c in range(3):
                    next_indices(0, c)
                each_round(act, round_)
                for j in range(NODE_TILES - LAG, NODE_TILES):
                    finish(j, (added[1], NODE_TILES))
            with act.Else():
                for n in range(4):
                    nb = min(4, BLOCKS - 4 * n)
                    act.wait_ge(g_turned, n + 1)
                    nc.scalar.activation(g_dst_T[:, n * 512:n * 512 + nb * P], agg[n % 3][:, 0:nb * P],
                                         ACT.Copy).then_inc(g_turned_copied, 1)
                with act.Fori(0, TILES) as i:
                    act.wait_ge(g_xt_ready, i + 1)
                    nc.scalar.activation(g_rows_T[:, :], agg[0][:, 0:P], ACT.Copy).then_inc(g_xt_copied, 1)
                    act.wait_ge(g_sum_ready, i + 1)
                    nc.scalar.activation(g_sum[:, :], msg[:, 0:HID], ACT.Copy).then_inc(g_sum_copied, 1)
                with act.Fori(0, NODE_TILES) as j:
                    act.wait_ge(g_acc_turned, j + 1)
                    nc.scalar.activation(messages_T[:, ds(j * P, P)], agg[0][:, 0:P], ACT.Copy).then_inc(g_acc_copied, 1)
                each_node_tile(act, lambda j: finish(j, (g_acc_copied, NODE_TILES)))

        @block.vector
        def _(dve):
            steps = [0]

            def step(ins):
                steps[0] += 1
                ins.then_inc(prep, 1)
                dve.wait_ge(prep, steps[0])

            nc.vector.memset(first_dst[:], PAD_ROW).then_inc(filled, 1)
            nc.vector.memset(dst_rows[:, BLOCKS - 1, :], PAD_ROW).then_inc(filled, 1)
            nc.vector.memset(src_rows[:, BLOCKS - 1, :], 0).then_inc(filled, 1)
            nc.vector.memset(type_rows[:, BLOCKS - 1, :], 0).then_inc(filled, 1)
            nc.vector.memset(b_type[:], 0.0).then_inc(zeroed, 1)
            nc.vector.memset(b_wide[:], 0.0).then_inc(zeroed, 1)
            nc.vector.memset(messages_T[:], 0.0).then_inc(zeroed, 1)
            for c in range(3):
                nc.vector.memset(type_mask[c][:], 0.0)
            nc.vector.memset(zeros[:], 0.0).then_inc(zeroed, 1)
            step(nc.vector.memset(row0[:], 0.0))
            nc.vector.memset(row0[0:1, :], 1.0).then_inc(zeroed, 1)
            step(nc.vector.memset(gate_bias[:], 0.0))

            dve.wait_ge(dst_in, 48)
            nc.vector.tensor_tensor(rel_f[:, :, :], dst_rows[:, :, :], dst_rows[:, :, 0:1].broadcast_to([P, BLOCKS, P]),
                                    ALU.subtract).then_inc(rel_ready, 1)
            dve.wait_ge(rel_ready, 1)
            step(nc.vector.scalar_tensor_tensor(out=rel_real[:, :, :], in0=dst_rows[:, :, :], scalar=float(NODES),
                                                in1=rel_f[:, :, :], op0=ALU.is_lt, op1=ALU.mult))
            nc.vector.tensor_reduce(bad[:, 0:1], rel_real[:, :, :].rearrange("p b e -> p (b e)"), AX, ALU.max)
            step(nc.vector.tensor_reduce(bad[:, 1:2], rel_real[:, :, :].rearrange("p b e -> p (b e)"), AX, ALU.min))
            nc.vector.tensor_scalar(bad[:, 2:3], bad[:, 0:1], float(SPAN - 1), None, ALU.is_gt)
            nc.vector.tensor_scalar(bad[:, 3:4], bad[:, 1:2], 0.0, None, ALU.is_lt).then_inc(bad_ready, 1)

            dve.wait_ge(first_in, 16)
            dve.wait_ge(consts, N_CONSTS)
            first = first_dst[0:1, :].rearrange("p (i k) -> p i k", k=ROUND)
            off = offset[0:1, :].rearrange("p (i k) -> p i k", k=ROUND)
            for c, n in enumerate(GROUPS):
                a = START[c]
                last = nc.vector.tensor_tensor(off[:, :, a:a + n], first[:, :, a:a + n],
                                               first[:, :, a:a + 1].broadcast_to([1, NODE_TILES, n]), ALU.subtract)
            nc.vector.tensor_tensor(rising[0:1, 0:ROW - 1], first_dst[0:1, 1:ROW], first_dst[0:1, 0:ROW - 1], ALU.subtract)
            step(nc.vector.tensor_tensor(ahead[0:1, :], first[:, :, 0], bound[0:1, :], ALU.subtract))
            nc.vector.tensor_reduce(checks[0:1, 0:1], offset[0:1, :], AX, ALU.max)
            nc.vector.tensor_reduce(checks[0:1, 1:2], rising[0:1, 0:ROW - 1], AX, ALU.min)
            step(nc.vector.tensor_reduce(checks[0:1, 2:3], ahead[0:1, :], AX, ALU.min))
            nc.vector.tensor_scalar(checks[0:1, 3:4], checks[0:1, 0:1], float(WINDOW - SPAN), None, ALU.is_le)
            step(nc.vector.tensor_scalar(checks[0:1, 4:6], checks[0:1, 1:3], 0.0, None, ALU.is_ge))
            step(nc.vector.tensor_tensor(checks[0:1, 6:7], checks[0:1, 4:5], checks[0:1, 5:6], ALU.mult))
            step(nc.vector.tensor_tensor(checks[0:1, 7:8], checks[0:1, 3:4], checks[0:1, 6:7], ALU.mult))
            dve.wait_ge(bad_summed, 1)
            step(nc.vector.tensor_reduce(checks[0:1, 0:1], xt[0:1, 0:2], AX, ALU.add))
            nc.vector.scalar_tensor_tensor(out=fits[0:1, 0:1], in0=checks[0:1, 0:1], scalar=0.5,
                                           in1=checks[0:1, 7:8], op0=ALU.is_lt, op1=ALU.mult).then_inc(fits_ready, 1)

            nc.vector.tensor_copy(iota_f[:, :], iota_i[:, :])
            step(nc.vector.tensor_copy(spare_f[:, :], spare_i[:, :]))
            dve.wait_ge(weights_in, 7 * 16)
            nc.vector.tensor_tensor(gate_bias[0:1, 0:2 * HID], bi_row[0:1, 0:2 * HID], bh_row[0:1, 0:2 * HID], ALU.add)
            nc.vector.tensor_copy(gate_bias[0:1, 2 * HID:3 * HID], bi_row[0:1, 2 * HID:GATE])
            step(nc.vector.tensor_copy(gate_bias[0:1, 3 * HID:4 * HID], bh_row[0:1, 2 * HID:GATE]))
            nc.vector.memset(checks[0:1, 0:1], 0.0).then_inc(zeroed, 1)

            def masks(r, c):
                n, a = GROUPS[c], r * ROUND + START[c]
                wait_used(dve, tiles_done[c], r)
                nc.vector.tensor_tensor(
                    node_mask[c][:, :, :], rel_T[:, ds(a, n)].unsqueeze(2).broadcast_to([P, n, SPAN]),
                    iota_f[:, :].unsqueeze(1).broadcast_to([P, n, SPAN]), ALU.is_equal).then_inc(node_mask_ready[c], 1)
                nc.vector.tensor_tensor(
                    type_mask[c][:, :, 0:TYPES], type_T[:, ds(a, n)].unsqueeze(2).broadcast_to([P, n, TYPES]),
                    iota_f[:, 0:TYPES].unsqueeze(1).broadcast_to([P, n, TYPES]),
                    ALU.is_equal).then_inc(type_mask_ready[c], 1)
                dve.wait_ge(node_mask_ready[c], r + 1)
                dve.wait_ge(type_mask_ready[c], r + 1)
                nc.vector.tensor_tensor(
                    onehot[c][:, :, :, :], node_mask[c][:, :, :].unsqueeze(3).broadcast_to([P, n, SPAN, TYPES]),
                    type_mask[c][:, :, 0:TYPES].unsqueeze(2).broadcast_to([P, n, SPAN, TYPES]),
                    ALU.mult).then_inc(onehot_ready[c], 1)

            def add_messages(r, c):
                a = r * ROUND + START[c]
                node = nc.values_load(first_dst[0:1, ds(a, 1)], engines=[dve.engine], min_val=0, max_val=NODES - 1,
                                      skip_runtime_bounds_check_because="a dst of a real edge")
                dve.wait_ge(applied[c], r + 1)
                nc.vector.tensor_tensor(messages_T[:, ds(node, WINDOW)], messages_T[:, ds(node, WINDOW)],
                                        msg[:, 0:WINDOW], ALU.add).then_inc(added[c], 1)

            def inverse_root(j):
                nc.vector.tensor_scalar(var_eps[:, :], mean_var[:, 1:2], EPS, None, ALU.add).then_inc(root_step[0], 1)
                dve.wait_ge(root_step[0], j + 1)
                nc.vector.tensor_scalar(half_bits[:, :], var_eps[:, :].bitcast(I32), 1, None,
                                        ALU.logical_shift_right).then_inc(root_step[1], 1)
                dve.wait_ge(root_step[1], j + 1)
                nc.vector.tensor_scalar(rstd[:, :].bitcast(I32), half_bits[:, :], -1.0, float(0x5F3759DF),
                                        ALU.mult, ALU.add).then_inc(root_step[2], 1)
                dve.wait_ge(root_step[2], j + 1)
                for n in range(NEWTON):
                    nc.vector.scalar_tensor_tensor(out=root_a[:, :], in0=rstd[:, :], scalar=rstd[:, 0:1], in1=var_eps[:, :],
                                                   op0=ALU.mult, op1=ALU.mult).then_inc(root_step[3 + 3 * n], 1)
                    dve.wait_ge(root_step[3 + 3 * n], j + 1)
                    nc.vector.tensor_scalar(root_b[:, :], root_a[:, :], -0.5, 1.5, ALU.mult, ALU.add).then_inc(root_step[4 + 3 * n], 1)
                    dve.wait_ge(root_step[4 + 3 * n], j + 1)
                    nc.vector.tensor_tensor(rstd[:, :], rstd[:, :], root_b[:, :], ALU.mult).then_inc(root_step[5 + 3 * n], 1)
                    dve.wait_ge(root_step[5 + 3 * n], j + 1)

            def finish(j):
                dve.wait_ge(rz_ready, j + 1)
                nc.vector.tensor_tensor(t_rh[:, :], rz[:, 0:HID], gates[:, 3 * HID:4 * HID], ALU.mult).then_inc(rh_ready, 1)
                dve.wait_ge(rh_ready, j + 1)
                nc.vector.tensor_tensor(t_pre[:, :], t_rh[:, :], gates[:, 2 * HID:3 * HID], ALU.add).then_inc(pre_ready, 1)
                dve.wait_ge(n_ready, j + 1)
                nc.vector.tensor_tensor(t_d[:, :], x_tile[:, :], t_n[:, :], ALU.subtract).then_inc(d_ready, 1)
                dve.wait_ge(d_ready, j + 1)
                nc.vector.tensor_tensor(t_zd[:, :], t_d[:, :], rz[:, HID:2 * HID], ALU.mult).then_inc(zd_ready, 1)
                dve.wait_ge(zd_ready, j + 1)
                nc.vector.tensor_tensor(t_h[:, :], t_zd[:, :], t_n[:, :], ALU.add).then_inc(h_ready, 1)
                dve.wait_ge(h_ready, j + 1)
                nc.vector.tensor_tensor(t_y[:, :], t_h[:, :], x_tile[:, :], ALU.add).then_inc(y_ready, 1)
                dve.wait_ge(y_ready, j + 1)
                nc.vector.bn_stats(stats[:, :], t_y[:, :]).then_inc(stats_ready, 1)
                dve.wait_ge(fits_ready, 1)
                dve.wait_ge(stats_ready, j + 1)
                nc.vector.bn_aggr(mean_var[:, :], stats[:, :]).then_inc(mv_ready, 1)
                dve.wait_ge(mv_ready, j + 1)
                inverse_root(j)
                wait_used(dve, out_stored, j * 16)
                nc.vector.tensor_scalar(out_tile[:, :], t_y[:, :], mean_var[:, 0:1], rstd[:, 0:1],
                                        ALU.subtract, ALU.mult).then_inc(out_ready, 1)

            def round_(r, fin, last):
                masks(r, 1)
                if not (isinstance(r, int) and r == 0):
                    add_messages(r - 1, 2)
                if fin:
                    finish(r - LAG)
                if not last:
                    masks(r, 2)
                add_messages(r, 0)
                if not last:
                    masks(r + 1, 0)
                    add_messages(r, 1)

            flag = load_flag(dve)
            with dve.If(flag):
                dve.wait_ge(turned_copied, len(TURNS))
                masks(0, 0)
                each_round(dve, round_)
                add_messages(NODE_TILES - 1, 1)
                for j in range(NODE_TILES - LAG, NODE_TILES):
                    finish(j)
            with dve.Else():
                dve.wait_ge(turned_copied, len(TURNS))
                nc.vector.tensor_copy(rel_f[:, :, :], dst_rows[:, :, :]).then_inc(g_dst_f, 1)
                dve.wait_ge(g_turned_copied, 4)
                STEPS = 6 + TYPES
                with dve.Fori(0, TILES) as i:
                    done = [0]

                    def g(ins):
                        done[0] += 1
                        ins.then_inc(g_step, 1)
                        dve.wait_ge(g_step, i * STEPS + done[0])

                    dve.wait_ge(g_added, (i + 1) * 16)
                    nc.vector.tensor_copy(g_idx[:, :], src_T[:, ds(i, 1)]).then_inc(g_idx_ready, 1)
                    g(nc.vector.tensor_copy(g_col[:, :], g_dst_T[:, ds(i, 1)]))
                    nc.vector.tensor_copy(g_wide[:, :], g_col[:, 0:1].broadcast_to([P, P])).then_inc(g_wide_ready, 1)
                    g(nc.vector.tensor_tensor(g_types[:, :], type_T[:, ds(i, 1)].broadcast_to([P, TYPES]),
                                              iota_f[:, 0:TYPES], ALU.is_equal))
                    dve.wait_ge(g_xt_ready, i + 1)
                    g(nc.vector.tensor_scalar(g_same[:, :], agg[1][:, 0:P], g_col[:, 0:1], None, ALU.is_equal))
                    g(nc.vector.tensor_tensor(g_before[:, :], g_same[:, :], earlier[:, :], ALU.mult))
                    g(nc.vector.tensor_reduce(g_n[:, :], g_before[:, :], AX, ALU.add))
                    nc.vector.tensor_scalar(g_first[:, :], g_n[:, :], 0.5, None, ALU.is_lt)
                    g(nc.vector.tensor_tensor(g_rise[:, :], g_col[:, :], spare_f[:, :], ALU.subtract))
                    nc.vector.scalar_tensor_tensor(out=g_row[:, :], in0=g_rise[:, :], scalar=g_first[:, 0:1],
                                                   in1=spare_f[:, :], op0=ALU.mult, op1=ALU.add)
                    dve.wait_ge(g_prod_ready, i + 1)
                    g(nc.vector.tensor_scalar(g_msg[:, :], agg[2][:, 0:HID], g_types[:, 0:1], None, ALU.mult))
                    for t in range(1, TYPES):
                        bank = agg[2] if t < 4 else cnt[0]
                        ins = nc.vector.scalar_tensor_tensor(
                            out=g_msg[:, :], in0=bank[:, t % 4 * HID:(t % 4 + 1) * HID], scalar=g_types[:, t:t + 1],
                            in1=g_msg[:, :], op0=ALU.mult, op1=ALU.add)
                        if t < TYPES - 1:
                            g(ins)
                    ins.then_inc(g_step, 1)
                    assert done[0] + 1 == STEPS
                    dve.wait_ge(g_step, (i + 1) * STEPS)
                    nc.vector.tensor_copy(g_types[:, 0:1], g_n[:, 0:1]).then_inc(g_msg_ready, 1)
                each_node_tile(dve, finish)

        @block.tensor
        def _(pe):
            pe.wait_ge(consts, N_CONSTS)
            pe.wait_ge(bad_ready, 1)
            nc.tensor.matmul(xt[:, 0:2], ones[:, :], bad[:, 2:4], start=True, stop=True).then_inc(bad_summed, 1)
            for n, (a, b0, nb) in enumerate(TURNS):
                if n < 3:
                    pass
                else:
                    pe.wait_ge(turned_copied, n - 2)
                pe.wait_ge((src_f_ready, rel_ready, type_f_ready)[a], 1)
                for b in range(nb):
                    last = nc.tensor.transpose(agg[n % 3][:, b * P:(b + 1) * P],
                                               (src_f, rel_f, type_f)[a][:, b0 + b, :], ident[:, :])
                last.then_inc(turned, 1)
            pe.wait_ge(weights_in, 7 * 16)
            for bank, w in ((gates, w_ih_rows), (msg, w_hh_rows)):
                for a in range(3):
                    last = nc.tensor.transpose(bank[:, a * P:(a + 1) * P], w[:, a, :], ident[:, :])
                last.then_inc(turned, 1)
            pe.wait_ge(turned_copied, len(TURNS) + 2)
            pe.wait_ge(zeroed, N_ZEROED + 1)

            def sum_tiles(r, c):
                n, a = GROUPS[c], r * ROUND + START[c]
                counts_bank = cnt[c % 2]
                _, offs = nc.values_load_multi_w_load_instructions(
                    offset[0:1, ds(a, n)], engines=[pe.engine], min_val=0, max_val=WINDOW - SPAN,
                    skip_runtime_bounds_check_because="checked on the chip before this path is taken")
                wait_used(pe, sums_copied[c], r)
                if c == 0:
                    wait_used(pe, sums_copied[2], r)
                if c == 2:
                    pe.wait_ge(sums_copied[0], r + 1)
                nc.tensor.matmul(agg[c][:, :], zeros[:, 0:P], zeros[:, :], start=True, stop=True)
                nc.tensor.matmul(counts_bank[:, 0:WINDOW], zeros[:, 0:P], zeros[:, 0:WINDOW], start=True, stop=True)
                pe.wait_ge(onehot_ready[c], r + 1)
                for k in range(n):
                    nc.tensor.matmul(counts_bank[:, ds(offs[k], SPAN)], type_mask[c][:, k, :], node_mask[c][:, k, :],
                                     start=False, stop=True, skip_group_check=True)
                    pe.wait_ge(gathered[START[c] + k], (r + 1) * 16)
                    last = nc.tensor.matmul(agg[c][:, ds(offs[k] * TYPES, SPAN * TYPES)], rows[:, START[c] + k, :],
                                            onehot[c][:, k, :, :].rearrange("p n t -> p (n t)"),
                                            start=False, stop=True, skip_group_check=True)
                last.then_inc(tiles_done[c], 1)

            def apply_weights(r, c):
                pe.wait_ge(sums_copied[c], r + 1)
                if c:
                    pe.wait_ge(added[c - 1], r + 1)
                elif not (isinstance(r, int) and r == 0):
                    pe.wait_ge(added[2], r)
                nc.tensor.matmul(msg[:, 0:WINDOW], b_type[:, :], counts[c][:, :], start=True, stop=False)
                for t in range(TYPES):
                    last = nc.tensor.matmul(msg[:, 0:WINDOW], w_type[:, t, :], sums[c][:, t, :],
                                            start=False, stop=t == TYPES - 1)
                last.then_inc(applied[c], 1)

            def finish(j):
                pe.wait_ge(x_in, (j + 1) * 16)
                nc.tensor.transpose(xt[:, 0:P], x_tile[:, :], ident[:, :]).then_inc(xt_ready, 1)
                wait_used(pe, pre_ready, j)
                nc.tensor.matmul(gates[:, :], row0[:, :], gate_bias[:, :], start=True, stop=False)
                pe.wait_ge(xt_copied, j + 1)
                nc.tensor.matmul(gates[:, 0:2 * HID], x_T[:, :], w_hh_T[:, 0:2 * HID], start=False, stop=False)
                pe.wait_ge(messages_copied, j + 1)
                nc.tensor.matmul(gates[:, 0:GATE], messages[:, :], w_ih_T[:, :], start=False, stop=False)
                nc.tensor.matmul(gates[:, 3 * HID:4 * HID], x_T[:, :], w_hh_T[:, 2 * HID:GATE],
                                 start=False, stop=True).then_inc(gates_ready, 1)

            def round_(r, fin, last):
                sum_tiles(r, 0)
                if not (isinstance(r, int) and r == 0):
                    apply_weights(r - 1, 2)
                if fin:
                    finish(r - LAG)
                sum_tiles(r, 1)
                apply_weights(r, 0)
                if not last:
                    sum_tiles(r, 2)
                    apply_weights(r, 1)

            flag = load_flag(pe)
            with pe.If(flag):
                each_round(pe, round_)
                apply_weights(NODE_TILES - 1, 1)
                for j in range(NODE_TILES - LAG, NODE_TILES):
                    finish(j)
            with pe.Else():
                pe.wait_ge(g_dst_f, 1)
                for n in range(4):
                    if n == 3:
                        pe.wait_ge(g_turned_copied, 1)
                    for b in range(4 * n, min(4 * n + 4, BLOCKS)):
                        last = nc.tensor.transpose(agg[n % 3][:, (b % 4) * P:(b % 4 + 1) * P], rel_f[:, b, :], ident[:, :])
                    last.then_inc(g_turned, 1)
                pe.wait_ge(g_turned_copied, 4)
                with pe.Fori(0, TILES) as i:
                    pe.wait_ge(g_wide_ready, i + 1)
                    nc.tensor.transpose(agg[1][:, 0:P], g_wide[:, :], ident[:, :])
                    pe.wait_ge(g_gathered, (i + 1) * 16)
                    nc.tensor.transpose(agg[0][:, 0:P], g_rows[:, :], ident[:, :]).then_inc(g_xt_ready, 1)
                    pe.wait_ge(g_xt_copied, i + 1)
                    for h, bank in enumerate((agg[2], cnt[0])):
                        cols = slice(h * 4 * HID, (h + 1) * 4 * HID)
                        nc.tensor.matmul(bank[:, :], row0[:, :], b_wide[:, cols], start=True, stop=False)
                        last = nc.tensor.matmul(bank[:, :], g_rows_T[:, :],
                                                w_type[:, 4 * h:4 * h + 4, :].rearrange("p t d -> p (t d)"),
                                                start=False, stop=True)
                    last.then_inc(g_prod_ready, 1)
                    pe.wait_ge(g_msg_ready, i + 1)
                    nc.tensor.matmul(msg[:, 0:HID], g_same[:, :], g_msg[:, :], start=True, stop=True).then_inc(g_sum_ready, 1)
                def turn_acc(j):
                    pe.wait_ge(g_acc_in, (j + 1) * 16)
                    wait_used(pe, g_acc_copied, j)
                    nc.tensor.transpose(agg[0][:, 0:P], g_acc[:, :], ident[:, :]).then_inc(g_acc_turned, 1)

                each_node_tile(pe, turn_acc)
                pe.wait_ge(g_acc_copied, NODE_TILES)
                each_node_tile(pe, finish)


_INS = ['x', 'src', 'dst', 'edge_type_8', 'L0_gnn_message_W', 'L0_gnn_message_b', 'L0_gnn_gru_w_ih',
        'L0_gnn_gru_w_hh', 'L0_gnn_gru_b_ih', 'L0_gnn_gru_b_hh']


def kernel(**inputs):
    import numpy as _np
    import concourse.bacc as _bacc
    from concourse import mybir as _mybir
    from concourse.bass_utils import run_bass_kernel_spmd as _run

    nc = _bacc.Bacc("TRN2", target_bir_lowering=False, num_devices=1)
    arrays, args = {}, []
    for name in _INS:
        a = _np.ascontiguousarray(inputs[name])
        arrays[f"in_{name}_dram"] = a
        args.append(nc.dram_tensor(f"in_{name}_dram", a.shape, _mybir.dt.from_np(a.dtype), kind="ExternalInput").ap())
    args.append(nc.dram_tensor("out_dram", arrays["in_x_dram"].shape, _mybir.dt.float32, kind="ExternalOutput").ap())
    gnn_kernel(nc, *args)
    r = _run(nc, [arrays], core_ids=[0])
    return r.results[0]["out_dram"]
```

```python
from contextlib import ExitStack

import concourse.bass as bass
from concourse import mybir

P = 128
F32 = mybir.dt.float32
BF16 = mybir.dt.bfloat16
I32 = mybir.dt.int32
ALU = mybir.AluOpType
ACT = mybir.ActivationFunctionType
AX = mybir.AxisListType.X
EPS = 1e-5
NEWTON = 3


def gnn_kernel(nc, x, src, dst, etype, w_msg, b_msg, w_ih, w_hh, b_ih, b_hh, out):
    ds = bass.ds
    NODES, HID = x.shape
    EDGES = src.shape[0]
    TYPES = w_msg.shape[0]
    TILES = -(-EDGES // P)
    NODE_TILES = -(-NODES // P)
    ROUND = -(-TILES // NODE_TILES)
    GROUPS = (6, 6, 5)
    START = (0, 6, 12)
    SPAN = 16
    WINDOW = 64
    LAG = 2
    LAST = TILES - (NODE_TILES - 1) * ROUND
    LAST_GROUPS = 2
    assert sum(GROUPS) == ROUND and LAST == GROUPS[0] + GROUPS[1] and HID == P
    BLOCKS = -(-TILES // P)
    FULL = EDGES // P - (BLOCKS - 1) * P
    REST = EDGES % P
    COLS = BLOCKS * P
    PAD_ROW = NODES + P
    ACC_ROWS = (NODE_TILES + 1) * P
    NODE_LAST = NODES - (NODE_TILES - 1) * P
    GATE = 3 * HID
    assert PAD_ROW < ACC_ROWS and NODES - 1 + WINDOW <= ACC_ROWS

    PARTS = 3
    CHUNK = 14
    ROWS_PP = NODES // P
    CHUNKS = -(-ROWS_PP // CHUNK)
    TAIL_ROWS = NODES - P * ROWS_PP
    LAST_CHUNK = ROWS_PP - (CHUNKS - 1) * CHUNK
    assert LAST_CHUNK + 1 <= CHUNK

    acc = nc.dram_tensor("message_rows", (ACC_ROWS, HID), F32, kind="Internal").ap()
    x_parts = nc.dram_tensor("x_parts", (NODES, PARTS * HID), BF16, kind="Internal").ap()

    ctx = ExitStack()
    with ctx:
        def sb(name, shape, dt=F32):
            return ctx.enter_context(nc.sbuf_tensor(name, shape, dt))

        def pb(name):
            return ctx.enter_context(nc.psum_tensor(name, [P, 512], F32))

        def sem(name):
            return ctx.enter_context(nc.semaphore(name))

        dst_rows = sb("dst_rows", [P, BLOCKS, P], I32)
        src_rows = sb("src_rows", [P, BLOCKS, P], I32)
        type_rows = sb("type_rows", [P, BLOCKS, P], I32)
        src_f = sb("src_f", [P, BLOCKS, P])
        type_f = sb("type_f", [P, BLOCKS, P])
        rel_f = sb("rel_f", [P, BLOCKS, P])
        rel_real = sb("rel_real", [P, BLOCKS, P])
        src_T = sb("src_T", [P, COLS])
        type_T = sb("type_T", [P, COLS])
        rel_T = sb("rel_T", [P, COLS])
        ROW = NODE_TILES * ROUND
        first_dst = sb("first_dst", [1, ROW], I32)
        offset = sb("offset", [1, ROW], I32)
        round_dst = sb("round_dst", [NODE_TILES, ROUND], I32)
        round_off = sb("round_off", [NODE_TILES, ROUND])
        round_rise = sb("round_rise", [NODE_TILES, ROUND])
        bound = sb("bound", [1, NODE_TILES], I32)
        ahead = sb("ahead", [1, NODE_TILES])
        seam = sb("seam", [1, NODE_TILES])
        extremes = sb("extremes", [P, 6])
        bad = sb("bad", [P, 6])
        bad_sum = sb("bad_sum", [1, 1])
        fits = sb("fits", [1, 1], I32)
        ident = sb("ident", [P, P])
        ones = sb("ones", [P, P])
        row0 = sb("row0", [P, P])
        earlier = sb("earlier", [P, P])
        iota_i = sb("iota_i", [P, SPAN], I32)
        iota_f = sb("iota_f", [P, SPAN])
        spare_i = sb("spare_i", [P, 1], I32)
        spare_f = sb("spare_f", [P, 1])
        w_type = sb("w_type", [P, TYPES, HID])
        b_type = sb("b_type", [P, HID])
        b_wide = sb("b_wide", [P, TYPES * HID])
        w_ih_rows = sb("w_ih_rows", [P, 3, HID])
        w_hh_rows = sb("w_hh_rows", [P, 3, HID])
        w_ih_T = sb("w_ih_T", [P, GATE])
        w_hh_T = sb("w_hh_T", [P, GATE])
        bi_row = sb("bi_row", [1, GATE])
        bh_row = sb("bh_row", [1, GATE])
        gate_bias = sb("gate_bias", [1, 512])
        bias_rest = sb("bias_rest", [1, 512])
        bias_part = [sb(f"bias_part{n}", [1, 512], BF16) for n in range(PARTS)]
        bias_parts = sb("bias_parts", [P, 512], BF16)
        rows012 = sb("rows012", [P, P], BF16)
        zeros_f = sb("zeros_f", [P, 512])
        idx = sb("idx", [P, ROUND], I32)
        rows = sb("rows", [P, ROUND, PARTS * HID], BF16)
        node_mask = [sb(f"node_mask{c}", [P, n, SPAN], BF16) for c, n in enumerate(GROUPS)]
        type_mask = [sb(f"type_mask{c}", [P, n, P], BF16) for c, n in enumerate(GROUPS)]
        onehot = [sb(f"onehot{c}", [P, n, SPAN, TYPES], BF16) for c, n in enumerate(GROUPS)]
        sums = sb("sums", [P, TYPES, 3, WINDOW])
        counts = sb("counts", [P, 3, WINDOW])
        messages_T = sb("messages_T", [P, ACC_ROWS])
        def under(first, n, dt=F32):
            view = messages_T[:, first:first + n]
            return (view if dt == F32 else view.bitcast(dt)).rearrange("p (a d) -> p a d", a=CHUNK)

        CW = CHUNK * HID
        x_chunk = [under(b * CW, CW) for b in range(2)]
        rest_chunk = [under((2 + b) * CW, CW) for b in range(2)]
        parts_chunk = [under(4 * CW + b * (CW * PARTS // 2), CW * PARTS // 2, BF16) for b in range(2)]
        assert 4 * CW + 2 * (CW * PARTS // 2) <= ACC_ROWS
        x_tile = sb("x_tile", [P, HID])
        x_T = sb("x_T", [P, P])
        messages = sb("messages", [P, P])
        rz = sb("rz", [P, 2 * HID])
        t_rh = sb("t_rh", [P, HID])
        t_pre = sb("t_pre", [P, HID])
        t_n = sb("t_n", [P, HID])
        t_d = sb("t_d", [P, HID])
        t_zd = sb("t_zd", [P, HID])
        t_h = sb("t_h", [P, HID])
        t_y = sb("t_y", [P, HID])
        stats = sb("stats", [P, nc.vector.BN_STATS_DIM])
        mean_var = sb("mean_var", [P, nc.vector.BN_AGGR_DIM])
        var_eps = sb("var_eps", [P, 1])
        half_bits = sb("half_bits", [P, 1], I32)
        root_a = sb("root_a", [P, 1])
        root_b = sb("root_b", [P, 1])
        rstd = sb("rstd", [P, 1])
        out_tile = sb("out_tile", [P, HID])
        g_dst_T = sb("g_dst_T", [P, COLS])
        g_idx = sb("g_idx", [P, 1], I32)
        g_col = sb("g_col", [P, 1])
        g_wide = sb("g_wide", [P, P])
        g_types = sb("g_types", [P, TYPES])
        g_rows = sb("g_rows", [P, HID])
        g_rows_T = sb("g_rows_T", [P, P])
        g_same = sb("g_same", [P, P])
        g_before = sb("g_before", [P, P])
        g_n = sb("g_n", [P, 1])
        g_first = sb("g_first", [P, 1])
        g_rise = sb("g_rise", [P, 1])
        g_row = sb("g_row", [P, 1], I32)
        g_msg = sb("g_msg", [P, HID])
        g_sum = sb("g_sum", [P, HID])
        g_acc = sb("g_acc", [P, HID])

        agg = [pb(f"agg{c}") for c in range(3)]
        cnt = [pb(f"cnt{c}") for c in range(2)]
        msg = pb("msg")
        gates = pb("gates")
        xt = pb("xt")

        filled = sem("filled")
        dst_in = sem("dst_in")
        first_in = sem("first_in")
        src_in = sem("src_in")
        type_in = sem("type_in")
        weights_in = sem("weights_in")
        consts = sem("consts")
        zeroed = sem("zeroed")
        prep = sem("prep")
        chunk_in = [sem(f"chunk_in{b}") for b in range(2)]
        hi_ready = sem("hi_ready")
        rest_ready = sem("rest_ready")
        mid_ready = sem("mid_ready")
        lo_ready = sem("lo_ready")
        chunk_out = [sem(f"chunk_out{b}") for b in range(2)]
        tail_in = sem("tail_in")
        tail_out = sem("tail_out")
        bias_split = sem("bias_split")
        bias_in = sem("bias_in")
        banks_zero = sem("banks_zero")
        messages_zero = sem("messages_zero")
        rel_ready = sem("rel_ready")
        src_f_ready = sem("src_f_ready")
        type_f_ready = sem("type_f_ready")
        turned = sem("turned")
        turned_copied = sem("turned_copied")
        bad_ready = sem("bad_ready")
        bad_summed = sem("bad_summed")
        fits_ready = sem("fits_ready")
        gathered = [sem(f"gathered{k}") for k in range(ROUND)]
        idx_ready = [sem(f"idx_ready{c}") for c in range(3)]
        node_mask_ready = [sem(f"node_mask_ready{c}") for c in range(3)]
        type_mask_ready = [sem(f"type_mask_ready{c}") for c in range(3)]
        onehot_ready = [sem(f"onehot_ready{c}") for c in range(3)]
        tiles_done = [sem(f"tiles_done{c}") for c in range(3)]
        sums_read = [sem(f"sums_read{c}") for c in range(3)]
        sums_copied = [sem(f"sums_copied{c}") for c in range(3)]
        applied = sem("applied")
        window_added = [sem(f"window_added{c}") for c in range(2)]
        added = sem("added")
        x_in = sem("x_in")
        xt_ready = sem("xt_ready")
        xt_copied = sem("xt_copied")
        messages_copied = sem("messages_copied")
        gates_ready = sem("gates_ready")
        rz_ready = sem("rz_ready")
        rh_ready = sem("rh_ready")
        pre_ready = sem("pre_ready")
        n_ready = sem("n_ready")
        d_ready = sem("d_ready")
        zd_ready = sem("zd_ready")
        h_ready = sem("h_ready")
        y_ready = sem("y_ready")
        stats_ready = sem("stats_ready")
        mv_ready = sem("mv_ready")
        root_step = [sem(f"root_step{n}") for n in range(3 + 3 * NEWTON)]
        out_ready = sem("out_ready")
        out_stored = sem("out_stored")
        g_dst_f = sem("g_dst_f")
        g_turned = sem("g_turned")
        g_turned_copied = sem("g_turned_copied")
        g_idx_ready = sem("g_idx_ready")
        g_col_ready = sem("g_col_ready")
        g_wide_ready = sem("g_wide_ready")
        g_gathered = sem("g_gathered")
        g_xt_ready = sem("g_xt_ready")
        g_xt_copied = sem("g_xt_copied")
        g_prod_ready = sem("g_prod_ready")
        g_step = sem("g_step")
        g_msg_ready = sem("g_msg_ready")
        g_sum_ready = sem("g_sum_ready")
        g_sum_copied = sem("g_sum_copied")
        g_added = sem("g_added")
        g_acc_in = sem("g_acc_in")
        g_acc_turned = sem("g_acc_turned")
        g_acc_copied = sem("g_acc_copied")

        block = ctx.enter_context(nc.Block())

        TURNS = [(a, b0, min(4, BLOCKS - b0)) for a in range(3) for b0 in range(0, BLOCKS, 4)]
        N_FILLED = 5
        N_CONSTS = 6
        N_ZEROED = 4

        def load_flag(engine):
            engine.wait_ge(fits_ready, 1)
            return nc.values_load(fits[0:1, 0:1], engines=[engine.engine], min_val=0, max_val=1,
                                  skip_runtime_bounds_check_because="it is a product of comparisons")

        def groups_of(last):
            return range(LAST_GROUPS if last else 3)

        def each_round(engine, body):
            for r in range(LAG + 1):
                body(r, r == LAG, False)
            with engine.Fori(LAG + 1, NODE_TILES - 2) as r:
                body(r, True, False)
            body(NODE_TILES - 2, True, False)
            body(NODE_TILES - 1, True, True)

        def each_node_tile(engine, body):
            body(0)
            with engine.Fori(1, NODE_TILES) as j:
                body(j)

        def wait_used(engine, semaphore, count):
            if not (isinstance(count, int) and count == 0):
                engine.wait_ge(semaphore, count)

        @block.sync
        def _(sp):
            def chunk_rows(table, n):
                whole = table[0:P * ROWS_PP, :].rearrange("(p a) d -> p a d", p=P)
                return whole[:, n * CHUNK:min((n + 1) * CHUNK, ROWS_PP), :]

            def load_chunk(n):
                if n >= 2:
                    sp.wait_ge(rest_ready, n - 1)
                k = LAST_CHUNK if n == CHUNKS - 1 else CHUNK
                sp.dma_start(x_chunk[n % 2][:, 0:k, :], chunk_rows(x, n)).then_inc(chunk_in[n % 2], 16)
                if n == CHUNKS - 1:
                    sp.dma_start(x_chunk[n % 2][0:TAIL_ROWS, k, :], x[P * ROWS_PP:NODES, :]).then_inc(tail_in, 16)

            def store_chunk(n):
                sp.wait_ge(lo_ready, n + 1)
                k = LAST_CHUNK if n == CHUNKS - 1 else CHUNK
                sp.dma_start(chunk_rows(x_parts, n), parts_chunk[n % 2][:, 0:k, :]).then_inc(chunk_out[n % 2], 16)
                if n == CHUNKS - 1:
                    sp.dma_start(x_parts[P * ROWS_PP:NODES, :],
                                 parts_chunk[n % 2][0:TAIL_ROWS, k, :]).then_inc(tail_out, 16)

            load_chunk(0)
            load_chunk(1)
            for n in range(CHUNKS):
                if n + 2 < CHUNKS:
                    load_chunk(n + 2)
                store_chunk(n)
            sp.wait_ge(bias_split, 1)
            for n in range(PARTS):
                sp.dma_start(bias_parts[n:n + 1, :], bias_part[n][0:1, :]).then_inc(bias_in, 16)

            def load_x(j, n=P):
                sp.dma_start(x_tile[0:n, :], x[ds(j * P, n), :]).then_inc(x_in, 16)

            def store_out(j, n=P):
                sp.wait_ge(out_ready, j + 1)
                sp.dma_start(out[ds(j * P, n), :], out_tile[0:n, :]).then_inc(out_stored, 16)

            def node_tiles():
                load_x(0)
                with sp.Fori(0, NODE_TILES - 2) as j:
                    store_out(j)
                    load_x(j + 1)
                store_out(NODE_TILES - 2)
                load_x(NODE_TILES - 1, NODE_LAST)
                store_out(NODE_TILES - 1, NODE_LAST)
                sp.wait_ge(out_stored, 16 * NODE_TILES)

            flag = load_flag(sp)
            with sp.If(flag):
                node_tiles()
            with sp.Else():
                sp.wait_ge(g_added, 16 * (TILES + 1))
                def load_acc(j):
                    wait_used(sp, g_acc_copied, j)
                    sp.dma_start(g_acc[:, :], acc[ds(j * P, P), :]).then_inc(g_acc_in, 16)

                each_node_tile(sp, load_acc)
                node_tiles()

        @block.gpsimd
        def _(pool):
            nc.gpsimd.memset(ident[:], 0.0).then_inc(consts, 1)
            nc.gpsimd.memset(ones[:], 1.0).then_inc(consts, 1)
            nc.gpsimd.iota(iota_i[:], pattern=[[1, SPAN]], base=0, channel_multiplier=0).then_inc(consts, 1)
            nc.gpsimd.iota(bound[:], pattern=[[P, NODE_TILES]], base=-P * (LAG - 1),
                           channel_multiplier=0).then_inc(consts, 1)
            nc.gpsimd.iota(spare_i[:], pattern=[[0, 1]], base=NODES, channel_multiplier=1).then_inc(consts, 1)
            pool.wait_ge(consts, 5)
            nc.gpsimd.affine_select(out=ident[:], in_=ident[:], compare_op=ALU.not_equal, fill=1.0, base=0,
                                    pattern=[[-1, P]], channel_multiplier=1)
            nc.gpsimd.affine_select(out=earlier[:], in_=ones[:], compare_op=ALU.is_gt, fill=0.0, base=0,
                                    pattern=[[-1, P]], channel_multiplier=1).then_inc(consts, 1)

            def gather_round(due, last=False):
                for c in groups_of(last):
                    pool.wait_ge(fits_ready, 1)
                    pool.wait_ge(idx_ready[c], due)
                    for k in range(START[c], START[c] + GROUPS[c]):
                        nc.gpsimd.indirect_dma_start(
                            out=rows[:, k, :], out_offset=None, in_=x_parts[:, :],
                            in_offset=bass.IndirectOffsetOnAxis(ap=idx[:, k:k + 1], axis=0),
                        ).then_inc(gathered[k], 16)

            flag = load_flag(pool)
            with pool.If(flag):
                for b in range(2):
                    pool.wait_ge(chunk_out[b], 16 * len(range(b, CHUNKS, 2)))
                pool.wait_ge(tail_out, 16)
                with pool.Fori(1, NODE_TILES) as due:
                    gather_round(due)
                gather_round(NODE_TILES, last=True)
            with pool.Else():
                pool.wait_ge(messages_zero, 1)
                nc.gpsimd.dma_start(acc.rearrange("(p r) d -> p (r d)", p=P), messages_T[:, :]).then_inc(g_added, 16)
                pool.wait_ge(g_added, 16)
                with pool.Fori(1, TILES + 1) as due:
                    pool.wait_ge(fits_ready, 1)
                    pool.wait_ge(g_idx_ready, due)
                    nc.gpsimd.indirect_dma_start(
                        out=g_rows[:, :], out_offset=None, in_=x[:, :],
                        in_offset=bass.IndirectOffsetOnAxis(ap=g_idx[:, 0:1], axis=0),
                    ).then_inc(g_gathered, 16)
                    pool.wait_ge(fits_ready, 1)
                    pool.wait_ge(g_sum_copied, due)
                    nc.gpsimd.indirect_dma_start(
                        out=acc[:, :], out_offset=bass.IndirectOffsetOnAxis(ap=g_row[:, 0:1], axis=0),
                        in_=g_sum[:, :], in_offset=None, compute_op=ALU.add,
                    ).then_inc(g_added, 16)
                    pool.wait_ge(g_added, (due + 1) * 16)

        @block.scalar
        def _(act):
            def load_rows(tile, values, done):
                whole = (BLOCKS - 1) * P * P
                act.dma_start(tile[:, 0:BLOCKS - 1, :],
                              values[0:whole].rearrange("(b p e) -> p b e", p=P, e=P)).then_inc(done, 16)
                act.dma_start(tile[0:FULL, BLOCKS - 1, :],
                              values[whole:whole + FULL * P].rearrange("(p e) -> p e", e=P)).then_inc(done, 16)
                act.dma_start(tile[FULL:FULL + 1, BLOCKS - 1, 0:REST],
                              values[EDGES - REST:EDGES].rearrange("(p e) -> p e", p=1)).then_inc(done, 16)

            act.wait_ge(filled, N_FILLED)
            load_rows(dst_rows, dst, dst_in)
            with nc.allow_non_contiguous_dma(reason="the first dst of every edge tile, once"):
                act.dma_start(first_dst[0:1, 0:TILES],
                              dst[0:EDGES:P].rearrange("(p e) -> p e", p=1)).then_inc(first_in, 16)
                lot = (NODE_TILES - 2) * ROUND * P
                act.dma_start(round_dst[0:NODE_TILES - 2, :],
                              dst[0:lot:P].rearrange("(i k) -> i k", k=ROUND)).then_inc(first_in, 16)
                act.dma_start(round_dst[NODE_TILES - 2:NODE_TILES - 1, :],
                              dst[lot:lot + ROUND * P:P].rearrange("(i k) -> i k", i=1)).then_inc(first_in, 16)
                act.dma_start(round_dst[NODE_TILES - 1:NODE_TILES, 0:LAST],
                              dst[lot + ROUND * P:EDGES:P].rearrange("(i k) -> i k", i=1)).then_inc(first_in, 16)
            load_rows(src_rows, src, src_in)
            load_rows(type_rows, etype, type_in)
            act.wait_ge(zeroed, N_ZEROED)
            act.dma_start(w_type[:, :, :], w_msg.rearrange("t h d -> h t d")).then_inc(weights_in, 16)
            act.dma_start(b_type[0:TYPES, :], b_msg).then_inc(weights_in, 16)
            act.dma_start(b_wide[0:1, :], b_msg.rearrange("(o t) d -> o (t d)", o=1)).then_inc(weights_in, 16)
            act.dma_start(w_ih_rows[:, :, :], w_ih.rearrange("(a p) h -> p a h", p=P)).then_inc(weights_in, 16)
            act.dma_start(w_hh_rows[:, :, :], w_hh.rearrange("(a p) h -> p a h", p=P)).then_inc(weights_in, 16)
            act.dma_start(bi_row[0:1, :], b_ih.rearrange("(o n) -> o n", o=1)).then_inc(weights_in, 16)
            act.dma_start(bh_row[0:1, :], b_hh.rearrange("(o n) -> o n", o=1)).then_inc(weights_in, 16)

            def hi_part(n):
                act.wait_ge(chunk_in[n % 2], 16 * (n // 2 + 1))
                if n == CHUNKS - 1:
                    act.wait_ge(tail_in, 16)
                if n >= 2:
                    act.wait_ge(chunk_out[n % 2], 16 * (n // 2))
                nc.scalar.activation(parts_chunk[n % 2][:, :, 0:HID], x_chunk[n % 2][:, :, :],
                                     ACT.Copy).then_inc(hi_ready, 1)

            def mid_part(n):
                act.wait_ge(rest_ready, n + 1)
                nc.scalar.activation(parts_chunk[n % 2][:, :, HID:2 * HID], rest_chunk[n % 2][:, :, :],
                                     ACT.Copy).then_inc(mid_ready, 1)

            def copy_turned(n):
                a, b0, nb = TURNS[n]
                act.wait_ge(turned, n + 1)
                nc.scalar.activation((src_T, rel_T, type_T)[a][:, b0 * P:(b0 + nb) * P],
                                     agg[n % 3][:, 0:nb * P], ACT.Copy).then_inc(turned_copied, 1)

            hi_part(0)
            hi_part(1)
            act.wait_ge(src_in, 48)
            nc.scalar.activation(src_f[:, :, :], src_rows[:, :, :], ACT.Copy).then_inc(src_f_ready, 1)
            mid_part(0)
            act.wait_ge(type_in, 48)
            nc.scalar.activation(type_f[:, :, :], type_rows[:, :, :], ACT.Copy).then_inc(type_f_ready, 1)
            for n in range(2, CHUNKS):
                hi_part(n)
                copy_turned(2 * n - 4)
                mid_part(n - 1)
                copy_turned(2 * n - 3)
            mid_part(CHUNKS - 1)
            for n in range(2 * CHUNKS - 4, len(TURNS)):
                copy_turned(n)
            act.wait_ge(turned, len(TURNS) + 2)
            nc.scalar.activation(w_ih_T[:, :], gates[:, 0:GATE], ACT.Copy).then_inc(turned_copied, 1)
            nc.scalar.activation(w_hh_T[:, :], msg[:, 0:GATE], ACT.Copy).then_inc(turned_copied, 1)

            def next_indices(r, c):
                a = r * ROUND + START[c]
                nc.scalar.activation(idx[:, START[c]:START[c] + GROUPS[c]], src_T[:, ds(a, GROUPS[c])],
                                     ACT.Copy).then_inc(idx_ready[c], 1)

            def zero_banks(c):
                nc.scalar.activation(agg[c][:, :], zeros_f[:, :], ACT.Copy)
                return nc.scalar.activation(cnt[c % 2][:, 0:WINDOW], zeros_f[:, 0:WINDOW], ACT.Copy)

            def copy_sums(r, c, more):
                act.wait_ge(tiles_done[c], r + 1)
                if more:
                    next_indices(r + 1, c)
                wait_used(act, applied, r)
                nc.scalar.activation(sums[:, :, c, :],
                                     agg[c][:, :].rearrange("p (n t) -> p t n", t=TYPES), ACT.Copy)
                nc.scalar.activation(counts[:, c, :], cnt[c % 2][:, 0:WINDOW], ACT.Copy).then_inc(sums_read[c], 1)
                act.wait_ge(sums_read[c], r + 1)
                zero_banks(c).then_inc(sums_copied[c], 1)

            def finish_copies(j, nodes_added):
                act.wait_ge(xt_ready, j + 1)
                wait_used(act, gates_ready, j)
                nc.scalar.activation(x_T[:, :], xt[:, 0:P], ACT.Copy).then_inc(xt_copied, 1)
                act.wait_ge(*nodes_added)
                nc.scalar.activation(messages[:, :], messages_T[:, ds(j * P, P)], ACT.Copy).then_inc(messages_copied, 1)

            def finish_rz(j):
                act.wait_ge(gates_ready, j + 1)
                wait_used(act, out_ready, j)
                nc.scalar.activation(rz[:, :], gates[:, 0:2 * HID], ACT.Sigmoid).then_inc(rz_ready, 1)

            def finish_n(j):
                act.wait_ge(pre_ready, j + 1)
                nc.scalar.activation(t_n[:, :], t_pre[:, :], ACT.Tanh).then_inc(n_ready, 1)

            def finish(j, nodes_added):
                finish_copies(j, nodes_added)
                finish_rz(j)
                finish_n(j)

            def round_(r, fin, last):
                more = (lambda c: not last) if not isinstance(r, int) else (lambda c: r + 1 < NODE_TILES - 1 or (not last and c < LAST_GROUPS))
                copy_sums(r, 0, more(0))
                if fin:
                    finish_copies(r - LAG, (added, r))
                copy_sums(r, 1, more(1))
                if fin:
                    finish_rz(r - LAG)
                if not last:
                    copy_sums(r, 2, more(2))
                if fin:
                    finish_n(r - LAG)

            flag = load_flag(act)
            with act.If(flag):
                act.wait_ge(turned_copied, len(TURNS))
                zero_banks(0)
                zero_banks(1)
                nc.scalar.activation(agg[2][:, :], zeros_f[:, :], ACT.Copy).then_inc(banks_zero, 1)
                for c in range(3):
                    next_indices(0, c)
                each_round(act, round_)
                for j in range(NODE_TILES - LAG, NODE_TILES):
                    finish(j, (added, NODE_TILES))
            with act.Else():
                for n in range(4):
                    nb = min(4, BLOCKS - 4 * n)
                    act.wait_ge(g_turned, n + 1)
                    nc.scalar.activation(g_dst_T[:, n * 512:n * 512 + nb * P], agg[n % 3][:, 0:nb * P],
                                         ACT.Copy).then_inc(g_turned_copied, 1)
                with act.Fori(0, TILES) as i:
                    act.wait_ge(g_xt_ready, i + 1)
                    nc.scalar.activation(g_rows_T[:, :], agg[0][:, 0:P], ACT.Copy).then_inc(g_xt_copied, 1)
                    act.wait_ge(g_sum_ready, i + 1)
                    nc.scalar.activation(g_sum[:, :], msg[:, 0:HID], ACT.Copy).then_inc(g_sum_copied, 1)
                with act.Fori(0, NODE_TILES) as j:
                    act.wait_ge(g_acc_turned, j + 1)
                    nc.scalar.activation(messages_T[:, ds(j * P, P)], agg[0][:, 0:P], ACT.Copy).then_inc(g_acc_copied, 1)
                each_node_tile(act, lambda j: finish(j, (g_acc_copied, NODE_TILES)))

        @block.vector
        def _(dve):
            steps = [0]

            def step(ins):
                steps[0] += 1
                ins.then_inc(prep, 1)
                dve.wait_ge(prep, steps[0])

            nc.vector.memset(dst_rows[:, BLOCKS - 1, :], PAD_ROW).then_inc(filled, 1)
            nc.vector.memset(first_dst[0:1, TILES:ROW], PAD_ROW).then_inc(filled, 1)
            nc.vector.memset(round_dst[:, :], PAD_ROW).then_inc(filled, 1)
            nc.vector.memset(src_rows[:, BLOCKS - 1, :], 0).then_inc(filled, 1)
            nc.vector.memset(type_rows[:, BLOCKS - 1, :], 0).then_inc(filled, 1)
            nc.vector.memset(b_type[:], 0.0)
            nc.vector.memset(b_wide[:], 0.0)
            nc.vector.memset(bias_parts[:], 0.0)
            nc.vector.memset(zeros_f[:], 0.0).then_inc(zeroed, 1)
            for c in range(3):
                last = nc.vector.memset(type_mask[c][:], 0.0)
            last.then_inc(zeroed, 1)
            step(nc.vector.memset(row0[:], 0.0))
            nc.vector.memset(row0[0:1, :], 1.0).then_inc(zeroed, 1)
            step(nc.vector.memset(rows012[:], 0.0))
            nc.vector.memset(rows012[0:PARTS, :], 1.0).then_inc(zeroed, 1)
            step(nc.vector.memset(bad[:], 0.0))

            def rest_of(n):
                dve.wait_ge(hi_ready, n + 1)
                nc.vector.tensor_tensor(rest_chunk[n % 2][:, :, :], x_chunk[n % 2][:, :, :],
                                        parts_chunk[n % 2][:, :, 0:HID], ALU.subtract).then_inc(rest_ready, 1)

            def lo_part(n):
                dve.wait_ge(mid_ready, n + 1)
                nc.vector.tensor_tensor(parts_chunk[n % 2][:, :, 2 * HID:3 * HID], rest_chunk[n % 2][:, :, :],
                                        parts_chunk[n % 2][:, :, HID:2 * HID], ALU.subtract).then_inc(lo_ready, 1)

            def check_spans():
                dve.wait_ge(dst_in, 48)
                nc.vector.tensor_tensor(rel_f[:, :, :], dst_rows[:, :, :],
                                        dst_rows[:, :, 0:1].broadcast_to([P, BLOCKS, P]), ALU.subtract).then_inc(rel_ready, 1)
                dve.wait_ge(rel_ready, 1)
                step(nc.vector.scalar_tensor_tensor(out=rel_real[:, :, :], in0=dst_rows[:, :, :], scalar=float(NODES),
                                                    in1=rel_f[:, :, :], op0=ALU.is_lt, op1=ALU.mult))
                nc.vector.tensor_reduce(extremes[:, 0:1], rel_real[:, :, :].rearrange("p b e -> p (b e)"), AX, ALU.max)
                step(nc.vector.tensor_reduce(extremes[:, 1:2], rel_real[:, :, :].rearrange("p b e -> p (b e)"), AX, ALU.min))
                nc.vector.tensor_scalar(bad[:, 0:1], extremes[:, 0:1], float(SPAN - 1), None, ALU.is_gt)
                nc.vector.tensor_scalar(bad[:, 1:2], extremes[:, 1:2], 0.0, None, ALU.is_lt)

            def check_tiles():
                dve.wait_ge(first_in, 4 * 16)
                dve.wait_ge(consts, N_CONSTS)
                first = first_dst[0:1, :].rearrange("p (i k) -> p i k", k=ROUND)
                off = offset[0:1, :].rearrange("p (i k) -> p i k", k=ROUND)
                for c, n in enumerate(GROUPS):
                    a = START[c]
                    nc.vector.tensor_tensor(off[:, :, a:a + n], first[:, :, a:a + n],
                                            first[:, :, a:a + 1].broadcast_to([1, NODE_TILES, n]), ALU.subtract)
                    nc.vector.tensor_tensor(round_off[:, a:a + n], round_dst[:, a:a + n],
                                            round_dst[:, a:a + 1].broadcast_to([NODE_TILES, n]), ALU.subtract)
                nc.vector.tensor_tensor(round_rise[:, 0:ROUND - 1], round_dst[:, 1:ROUND], round_dst[:, 0:ROUND - 1], ALU.subtract)
                nc.vector.tensor_tensor(seam[0:1, 0:NODE_TILES - 1], first[:, 1:NODE_TILES, 0],
                                        first[:, 0:NODE_TILES - 1, ROUND - 1], ALU.subtract)
                step(nc.vector.tensor_tensor(ahead[0:1, :], first[:, :, 0], bound[0:1, :], ALU.subtract))
                nc.vector.tensor_reduce(extremes[0:NODE_TILES, 2:3], round_off[:, :], AX, ALU.max)
                nc.vector.tensor_reduce(extremes[0:NODE_TILES, 3:4], round_rise[:, 0:ROUND - 1], AX, ALU.min)
                nc.vector.tensor_reduce(extremes[0:1, 4:5], seam[0:1, 0:NODE_TILES - 1], AX, ALU.min)
                step(nc.vector.tensor_reduce(extremes[0:1, 5:6], ahead[0:1, :], AX, ALU.min))
                nc.vector.tensor_scalar(bad[0:NODE_TILES, 2:3], extremes[0:NODE_TILES, 2:3], float(WINDOW - SPAN), None, ALU.is_gt)
                nc.vector.tensor_scalar(bad[0:NODE_TILES, 3:4], extremes[0:NODE_TILES, 3:4], 0.0, None, ALU.is_lt)
                nc.vector.tensor_scalar(bad[0:1, 4:6], extremes[0:1, 4:6], 0.0, None, ALU.is_lt).then_inc(bad_ready, 1)

            def decide():
                dve.wait_ge(bad_summed, 1)
                step(nc.vector.tensor_reduce(bad_sum[0:1, 0:1], xt[0:1, 0:6], AX, ALU.add))
                nc.vector.tensor_scalar(fits[0:1, 0:1], bad_sum[0:1, 0:1], 0.5, None, ALU.is_lt).then_inc(fits_ready, 1)

            def split_bias():
                dve.wait_ge(weights_in, 7 * 16)
                nc.vector.tensor_tensor(gate_bias[0:1, 0:2 * HID], bi_row[0:1, 0:2 * HID], bh_row[0:1, 0:2 * HID], ALU.add)
                nc.vector.tensor_copy(gate_bias[0:1, 2 * HID:3 * HID], bi_row[0:1, 2 * HID:GATE])
                step(nc.vector.tensor_copy(gate_bias[0:1, 3 * HID:4 * HID], bh_row[0:1, 2 * HID:GATE]))
                step(nc.vector.tensor_copy(bias_part[0][0:1, :], gate_bias[0:1, :]))
                step(nc.vector.tensor_tensor(bias_rest[0:1, :], gate_bias[0:1, :], bias_part[0][0:1, :], ALU.subtract))
                step(nc.vector.tensor_copy(bias_part[1][0:1, :], bias_rest[0:1, :]))
                nc.vector.tensor_tensor(bias_part[2][0:1, :], bias_rest[0:1, :], bias_part[1][0:1, :],
                                        ALU.subtract).then_inc(bias_split, 1)

            def zero_messages():
                for b in range(2):
                    dve.wait_ge(chunk_out[b], 16 * len(range(b, CHUNKS, 2)))
                dve.wait_ge(tail_out, 16)
                nc.vector.memset(messages_T[:], 0.0).then_inc(messages_zero, 1)

            rest_of(0)
            check_spans()
            rest_of(1)
            lo_part(0)
            check_tiles()
            for n in range(2, CHUNKS):
                rest_of(n)
                lo_part(n - 1)
                if n == 2:
                    decide()
                if n == 3:
                    nc.vector.tensor_copy(iota_f[:, :], iota_i[:, :])
                    step(nc.vector.tensor_copy(spare_f[:, :], spare_i[:, :]))
                    split_bias()
            lo_part(CHUNKS - 1)

            def masks(r, c):
                n, a = GROUPS[c], r * ROUND + START[c]
                wait_used(dve, tiles_done[c], r)
                nc.vector.tensor_tensor(
                    node_mask[c][:, :, :], rel_T[:, ds(a, n)].unsqueeze(2).broadcast_to([P, n, SPAN]),
                    iota_f[:, :].unsqueeze(1).broadcast_to([P, n, SPAN]), ALU.is_equal).then_inc(node_mask_ready[c], 1)
                nc.vector.tensor_tensor(
                    type_mask[c][:, :, 0:TYPES], type_T[:, ds(a, n)].unsqueeze(2).broadcast_to([P, n, TYPES]),
                    iota_f[:, 0:TYPES].unsqueeze(1).broadcast_to([P, n, TYPES]),
                    ALU.is_equal).then_inc(type_mask_ready[c], 1)
                dve.wait_ge(node_mask_ready[c], r + 1)
                dve.wait_ge(type_mask_ready[c], r + 1)
                nc.vector.tensor_tensor(
                    onehot[c][:, :, :, :], node_mask[c][:, :, :].unsqueeze(3).broadcast_to([P, n, SPAN, TYPES]),
                    type_mask[c][:, :, 0:TYPES].unsqueeze(2).broadcast_to([P, n, SPAN, TYPES]),
                    ALU.mult).then_inc(onehot_ready[c], 1)

            def add_messages(r, groups=3):
                nodes = [nc.values_load(first_dst[0:1, ds(r * ROUND + START[c], 1)], engines=[dve.engine],
                                        min_val=0, max_val=NODES - 1,
                                        skip_runtime_bounds_check_because="a dst of a real edge")
                         for c in range(groups)]
                dve.wait_ge(applied, r + 1)
                for c, node in enumerate(nodes):
                    ins = nc.vector.tensor_tensor(messages_T[:, ds(node, WINDOW)], messages_T[:, ds(node, WINDOW)],
                                                  msg[:, c * WINDOW:(c + 1) * WINDOW], ALU.add)
                    if c < groups - 1:
                        ins.then_inc(window_added[c], 1)
                        dve.wait_ge(window_added[c], r + 1)
                ins.then_inc(added, 1)

            def inverse_root(j):
                nc.vector.tensor_scalar(var_eps[:, :], mean_var[:, 1:2], EPS, None, ALU.add).then_inc(root_step[0], 1)
                dve.wait_ge(root_step[0], j + 1)
                nc.vector.tensor_scalar(half_bits[:, :], var_eps[:, :].bitcast(I32), 1, None,
                                        ALU.logical_shift_right).then_inc(root_step[1], 1)
                dve.wait_ge(root_step[1], j + 1)
                nc.vector.tensor_scalar(rstd[:, :].bitcast(I32), half_bits[:, :], -1.0, float(0x5F3759DF),
                                        ALU.mult, ALU.add).then_inc(root_step[2], 1)
                dve.wait_ge(root_step[2], j + 1)
                for n in range(NEWTON):
                    nc.vector.scalar_tensor_tensor(out=root_a[:, :], in0=rstd[:, :], scalar=rstd[:, 0:1], in1=var_eps[:, :],
                                                   op0=ALU.mult, op1=ALU.mult).then_inc(root_step[3 + 3 * n], 1)
                    dve.wait_ge(root_step[3 + 3 * n], j + 1)
                    nc.vector.tensor_scalar(root_b[:, :], root_a[:, :], -0.5, 1.5, ALU.mult, ALU.add).then_inc(root_step[4 + 3 * n], 1)
                    dve.wait_ge(root_step[4 + 3 * n], j + 1)
                    nc.vector.tensor_tensor(rstd[:, :], rstd[:, :], root_b[:, :], ALU.mult).then_inc(root_step[5 + 3 * n], 1)
                    dve.wait_ge(root_step[5 + 3 * n], j + 1)

            def finish_pre(j):
                dve.wait_ge(rz_ready, j + 1)
                nc.vector.tensor_tensor(t_rh[:, :], rz[:, 0:HID], gates[:, 3 * HID:4 * HID], ALU.mult).then_inc(rh_ready, 1)
                dve.wait_ge(rh_ready, j + 1)
                nc.vector.tensor_tensor(t_pre[:, :], t_rh[:, :], gates[:, 2 * HID:3 * HID], ALU.add).then_inc(pre_ready, 1)

            def finish_out(j):
                dve.wait_ge(n_ready, j + 1)
                nc.vector.tensor_tensor(t_d[:, :], x_tile[:, :], t_n[:, :], ALU.subtract).then_inc(d_ready, 1)
                dve.wait_ge(d_ready, j + 1)
                nc.vector.tensor_tensor(t_zd[:, :], t_d[:, :], rz[:, HID:2 * HID], ALU.mult).then_inc(zd_ready, 1)
                dve.wait_ge(zd_ready, j + 1)
                nc.vector.tensor_tensor(t_h[:, :], t_zd[:, :], t_n[:, :], ALU.add).then_inc(h_ready, 1)
                dve.wait_ge(h_ready, j + 1)
                nc.vector.tensor_tensor(t_y[:, :], t_h[:, :], x_tile[:, :], ALU.add).then_inc(y_ready, 1)
                dve.wait_ge(y_ready, j + 1)
                nc.vector.bn_stats(stats[:, :], t_y[:, :]).then_inc(stats_ready, 1)
                dve.wait_ge(fits_ready, 1)
                dve.wait_ge(stats_ready, j + 1)
                nc.vector.bn_aggr(mean_var[:, :], stats[:, :]).then_inc(mv_ready, 1)
                dve.wait_ge(mv_ready, j + 1)
                inverse_root(j)
                wait_used(dve, out_stored, j * 16)
                nc.vector.tensor_scalar(out_tile[:, :], t_y[:, :], mean_var[:, 0:1], rstd[:, 0:1],
                                        ALU.subtract, ALU.mult).then_inc(out_ready, 1)

            def finish(j):
                finish_pre(j)
                finish_out(j)

            def round_(r, fin, last):
                first = isinstance(r, int) and r == 0
                if not first:
                    masks(r, 1)
                    add_messages(r - 1)
                    if not last:
                        masks(r, 2)
                if fin:
                    finish_pre(r - LAG)
                if not last:
                    masks(r + 1, 0)
                if fin:
                    finish_out(r - LAG)

            flag = load_flag(dve)
            with dve.If(flag):
                dve.wait_ge(turned_copied, len(TURNS))
                for c in range(3):
                    masks(0, c)
                zero_messages()
                each_round(dve, round_)
                add_messages(NODE_TILES - 1, LAST_GROUPS)
                for j in range(NODE_TILES - LAG, NODE_TILES):
                    finish(j)
            with dve.Else():
                dve.wait_ge(turned_copied, len(TURNS))
                nc.vector.tensor_copy(rel_f[:, :, :], dst_rows[:, :, :]).then_inc(g_dst_f, 1)
                zero_messages()
                dve.wait_ge(g_turned_copied, 4)
                STEPS = 6 + TYPES
                with dve.Fori(0, TILES) as i:
                    done = [0]

                    def g(ins):
                        done[0] += 1
                        ins.then_inc(g_step, 1)
                        dve.wait_ge(g_step, i * STEPS + done[0])

                    dve.wait_ge(g_added, (i + 1) * 16)
                    nc.vector.tensor_copy(g_idx[:, :], src_T[:, ds(i, 1)]).then_inc(g_idx_ready, 1)
                    g(nc.vector.tensor_copy(g_col[:, :], g_dst_T[:, ds(i, 1)]))
                    nc.vector.tensor_copy(g_wide[:, :], g_col[:, 0:1].broadcast_to([P, P])).then_inc(g_wide_ready, 1)
                    g(nc.vector.tensor_tensor(g_types[:, :], type_T[:, ds(i, 1)].broadcast_to([P, TYPES]),
                                              iota_f[:, 0:TYPES], ALU.is_equal))
                    dve.wait_ge(g_xt_ready, i + 1)
                    g(nc.vector.tensor_scalar(g_same[:, :], agg[1][:, 0:P], g_col[:, 0:1], None, ALU.is_equal))
                    g(nc.vector.tensor_tensor(g_before[:, :], g_same[:, :], earlier[:, :], ALU.mult))
                    g(nc.vector.tensor_reduce(g_n[:, :], g_before[:, :], AX, ALU.add))
                    nc.vector.tensor_scalar(g_first[:, :], g_n[:, :], 0.5, None, ALU.is_lt)
                    g(nc.vector.tensor_tensor(g_rise[:, :], g_col[:, :], spare_f[:, :], ALU.subtract))
                    nc.vector.scalar_tensor_tensor(out=g_row[:, :], in0=g_rise[:, :], scalar=g_first[:, 0:1],
                                                   in1=spare_f[:, :], op0=ALU.mult, op1=ALU.add)
                    dve.wait_ge(g_prod_ready, i + 1)
                    g(nc.vector.tensor_scalar(g_msg[:, :], agg[2][:, 0:HID], g_types[:, 0:1], None, ALU.mult))
                    for t in range(1, TYPES):
                        bank = agg[2] if t < 4 else cnt[0]
                        ins = nc.vector.scalar_tensor_tensor(
                            out=g_msg[:, :], in0=bank[:, t % 4 * HID:(t % 4 + 1) * HID], scalar=g_types[:, t:t + 1],
                            in1=g_msg[:, :], op0=ALU.mult, op1=ALU.add)
                        if t < TYPES - 1:
                            g(ins)
                    ins.then_inc(g_step, 1)
                    assert done[0] + 1 == STEPS
                    dve.wait_ge(g_step, (i + 1) * STEPS)
                    nc.vector.tensor_copy(g_types[:, 0:1], g_n[:, 0:1]).then_inc(g_msg_ready, 1)
                each_node_tile(dve, finish)

        @block.tensor
        def _(pe):
            pe.wait_ge(consts, N_CONSTS)
            for n, (a, b0, nb) in enumerate(TURNS):
                if n < 3:
                    pass
                else:
                    pe.wait_ge(turned_copied, n - 2)
                pe.wait_ge((src_f_ready, rel_ready, type_f_ready)[a], 1)
                for b in range(nb):
                    last = nc.tensor.transpose(agg[n % 3][:, b * P:(b + 1) * P],
                                               (src_f, rel_f, type_f)[a][:, b0 + b, :], ident[:, :])
                last.then_inc(turned, 1)
                if n == 3:
                    pe.wait_ge(bad_ready, 1)
                    nc.tensor.matmul(xt[:, 0:6], ones[:, :], bad[:, :], start=True, stop=True).then_inc(bad_summed, 1)
            pe.wait_ge(weights_in, 7 * 16)
            for bank, w in ((gates, w_ih_rows), (msg, w_hh_rows)):
                for a in range(3):
                    last = nc.tensor.transpose(bank[:, a * P:(a + 1) * P], w[:, a, :], ident[:, :])
                last.then_inc(turned, 1)
            pe.wait_ge(turned_copied, len(TURNS) + 2)
            pe.wait_ge(zeroed, N_ZEROED)
            pe.wait_ge(bias_in, PARTS * 16)

            def sum_tiles(r, c):
                n, a = GROUPS[c], r * ROUND + START[c]
                counts_bank = cnt[c % 2]
                _, offs = nc.values_load_multi_w_load_instructions(
                    offset[0:1, ds(a, n)], engines=[pe.engine], min_val=0, max_val=WINDOW - SPAN,
                    skip_runtime_bounds_check_because="checked on the chip before this path is taken")
                if isinstance(r, int) and r == 0:
                    pe.wait_ge(banks_zero, 1)
                else:
                    pe.wait_ge(sums_copied[c], r)
                    if c == 0:
                        pe.wait_ge(sums_copied[2], r)
                if c == 2:
                    pe.wait_ge(sums_copied[0], r + 1)
                pe.wait_ge(onehot_ready[c], r + 1)
                for k in range(n):
                    nc.tensor.matmul(counts_bank[:, ds(offs[k], SPAN)], type_mask[c][:, k, :], node_mask[c][:, k, :],
                                     start=False, stop=True, skip_group_check=True)
                    pe.wait_ge(gathered[START[c] + k], (r + 1) * 16)
                    for part in range(PARTS):
                        last = nc.tensor.matmul(agg[c][:, ds(offs[k] * TYPES, SPAN * TYPES)],
                                                rows[:, START[c] + k, part * HID:(part + 1) * HID],
                                                onehot[c][:, k, :, :].rearrange("p n t -> p (n t)"),
                                                start=False, stop=True, skip_group_check=True)
                last.then_inc(tiles_done[c], 1)

            def apply_weights(r, groups=3):
                pe.wait_ge(sums_copied[groups - 1], r + 1)
                wait_used(pe, added, r)
                out_cols = msg[:, 0:groups * WINDOW]
                nc.tensor.matmul(out_cols, b_type[:, :], counts[:, 0:groups, :].rearrange("p c n -> p (c n)"),
                                 start=True, stop=False)
                for t in range(TYPES):
                    last = nc.tensor.matmul(out_cols, w_type[:, t, :], sums[:, t, 0:groups, :].rearrange("p c n -> p (c n)"),
                                            start=False, stop=t == TYPES - 1)
                last.then_inc(applied, 1)

            def turn_x(j):
                pe.wait_ge(x_in, (j + 1) * 16)
                wait_used(pe, xt_copied, j)
                nc.tensor.transpose(xt[:, 0:P], x_tile[:, :], ident[:, :]).then_inc(xt_ready, 1)

            def make_gates(j):
                wait_used(pe, pre_ready, j)
                nc.tensor.matmul(gates[:, :], rows012[:, :], bias_parts[:, :], start=True, stop=False)
                pe.wait_ge(xt_copied, j + 1)
                nc.tensor.matmul(gates[:, 0:2 * HID], x_T[:, :], w_hh_T[:, 0:2 * HID], start=False, stop=False)
                nc.tensor.matmul(gates[:, 3 * HID:4 * HID], x_T[:, :], w_hh_T[:, 2 * HID:GATE], start=False, stop=False)
                pe.wait_ge(messages_copied, j + 1)
                nc.tensor.matmul(gates[:, 0:GATE], messages[:, :], w_ih_T[:, :], start=False, stop=True).then_inc(gates_ready, 1)

            def finish(j):
                turn_x(j)
                make_gates(j)

            def round_(r, fin, last):
                sum_tiles(r, 0)
                if fin:
                    turn_x(r - LAG)
                if not (isinstance(r, int) and r == 0):
                    apply_weights(r - 1)
                sum_tiles(r, 1)
                if fin:
                    make_gates(r - LAG)
                if not last:
                    sum_tiles(r, 2)

            flag = load_flag(pe)
            with pe.If(flag):
                each_round(pe, round_)
                apply_weights(NODE_TILES - 1, LAST_GROUPS)
                for j in range(NODE_TILES - LAG, NODE_TILES):
                    finish(j)
            with pe.Else():
                pe.wait_ge(g_dst_f, 1)
                for n in range(4):
                    if n == 3:
                        pe.wait_ge(g_turned_copied, 1)
                    for b in range(4 * n, min(4 * n + 4, BLOCKS)):
                        last = nc.tensor.transpose(agg[n % 3][:, (b % 4) * P:(b % 4 + 1) * P], rel_f[:, b, :], ident[:, :])
                    last.then_inc(g_turned, 1)
                pe.wait_ge(g_turned_copied, 4)
                with pe.Fori(0, TILES) as i:
                    pe.wait_ge(g_wide_ready, i + 1)
                    nc.tensor.transpose(agg[1][:, 0:P], g_wide[:, :], ident[:, :])
                    pe.wait_ge(g_gathered, (i + 1) * 16)
                    nc.tensor.transpose(agg[0][:, 0:P], g_rows[:, :], ident[:, :]).then_inc(g_xt_ready, 1)
                    pe.wait_ge(g_xt_copied, i + 1)
                    for h, bank in enumerate((agg[2], cnt[0])):
                        cols = slice(h * 4 * HID, (h + 1) * 4 * HID)
                        nc.tensor.matmul(bank[:, :], row0[:, :], b_wide[:, cols], start=True, stop=False)
                        last = nc.tensor.matmul(bank[:, :], g_rows_T[:, :],
                                                w_type[:, 4 * h:4 * h + 4, :].rearrange("p t d -> p (t d)"),
                                                start=False, stop=True)
                    last.then_inc(g_prod_ready, 1)
                    pe.wait_ge(g_msg_ready, i + 1)
                    nc.tensor.matmul(msg[:, 0:HID], g_same[:, :], g_msg[:, :], start=True, stop=True).then_inc(g_sum_ready, 1)
                def turn_acc(j):
                    pe.wait_ge(g_acc_in, (j + 1) * 16)
                    wait_used(pe, g_acc_copied, j)
                    nc.tensor.transpose(agg[0][:, 0:P], g_acc[:, :], ident[:, :]).then_inc(g_acc_turned, 1)

                each_node_tile(pe, turn_acc)
                pe.wait_ge(g_acc_copied, NODE_TILES)
                each_node_tile(pe, finish)


_INS = ['x', 'src', 'dst', 'edge_type_8', 'L0_gnn_message_W', 'L0_gnn_message_b', 'L0_gnn_gru_w_ih',
        'L0_gnn_gru_w_hh', 'L0_gnn_gru_b_ih', 'L0_gnn_gru_b_hh']


def kernel(**inputs):
    import numpy as _np
    import concourse.bacc as _bacc
    from concourse import mybir as _mybir
    from concourse.bass_utils import run_bass_kernel_spmd as _run

    nc = _bacc.Bacc("TRN2", target_bir_lowering=False, num_devices=1)
    arrays, args = {}, []
    for name in _INS:
        a = _np.ascontiguousarray(inputs[name])
        arrays[f"in_{name}_dram"] = a
        args.append(nc.dram_tensor(f"in_{name}_dram", a.shape, _mybir.dt.from_np(a.dtype), kind="ExternalInput").ap())
    args.append(nc.dram_tensor("out_dram", arrays["in_x_dram"].shape, _mybir.dt.float32, kind="ExternalOutput").ap())
    gnn_kernel(nc, *args)
    r = _run(nc, [arrays], core_ids=[0])
    return r.results[0]["out_dram"]
```

```python
from contextlib import ExitStack

import concourse.bass as bass
from concourse import mybir

P = 128
F32 = mybir.dt.float32
BF16 = mybir.dt.bfloat16
I32 = mybir.dt.int32
ALU = mybir.AluOpType
ACT = mybir.ActivationFunctionType
AX = mybir.AxisListType.X
EPS = 1e-5
NEWTON = 3


def gnn_kernel(nc, x, src, dst, etype, w_msg, b_msg, w_ih, w_hh, b_ih, b_hh, out):
    ds = bass.ds
    NODES, HID = x.shape
    EDGES = src.shape[0]
    TYPES = w_msg.shape[0]
    TILES = -(-EDGES // P)
    NODE_TILES = -(-NODES // P)
    ROUND = -(-TILES // NODE_TILES)
    GROUPS = (6, 6, 5)
    START = (0, 6, 12)
    SPAN = 16
    WINDOW = 64
    LAG = 2
    LAST = TILES - (NODE_TILES - 1) * ROUND
    LAST_GROUPS = 2
    assert sum(GROUPS) == ROUND and LAST == GROUPS[0] + GROUPS[1] and HID == P
    BLOCKS = -(-TILES // P)
    FULL = EDGES // P - (BLOCKS - 1) * P
    REST = EDGES % P
    COLS = BLOCKS * P
    PAD_ROW = NODES + P
    ACC_ROWS = (NODE_TILES + 1) * P
    NODE_LAST = NODES - (NODE_TILES - 1) * P
    GATE = 3 * HID
    assert PAD_ROW < ACC_ROWS and NODES - 1 + WINDOW <= ACC_ROWS

    ZERO_A, ZERO_B = 32 * P, 68 * P
    N_MESSAGES_ZERO = 3
    PARTS = 3

    acc = nc.dram_tensor("message_rows", (ACC_ROWS, HID), F32, kind="Internal").ap()

    ctx = ExitStack()
    with ctx:
        def sb(name, shape, dt=F32):
            return ctx.enter_context(nc.sbuf_tensor(name, shape, dt))

        def pb(name):
            return ctx.enter_context(nc.psum_tensor(name, [P, 512], F32))

        def sem(name):
            return ctx.enter_context(nc.semaphore(name))

        dst_rows = sb("dst_rows", [P, BLOCKS, P], I32)
        src_rows = sb("src_rows", [P, BLOCKS, P], I32)
        type_rows = sb("type_rows", [P, BLOCKS, P], I32)
        src_f = sb("src_f", [P, BLOCKS, P])
        type_f = sb("type_f", [P, BLOCKS, P])
        rel_f = sb("rel_f", [P, BLOCKS, P])
        src_T = sb("src_T", [P, COLS])
        type_T = sb("type_T", [P, COLS])
        rel_T = sb("rel_T", [P, COLS])
        ROW = NODE_TILES * ROUND
        first_dst = sb("first_dst", [1, ROW], I32)
        offset = sb("offset", [1, ROW], I32)
        round_dst = sb("round_dst", [NODE_TILES, ROUND], I32)
        round_off = sb("round_off", [NODE_TILES, ROUND])
        round_rise = sb("round_rise", [NODE_TILES, ROUND])
        bound = sb("bound", [1, NODE_TILES], I32)
        ahead = sb("ahead", [1, NODE_TILES])
        seam = sb("seam", [1, NODE_TILES])
        extremes = sb("extremes", [P, 10])
        bad = sb("bad", [P, 10])
        bad_sum = sb("bad_sum", [1, 1])
        fits = sb("fits", [1, 1], I32)
        ident = sb("ident", [P, P])
        ones = sb("ones", [P, P])
        row0 = sb("row0", [P, P])
        earlier = sb("earlier", [P, P])
        iota_i = sb("iota_i", [P, SPAN], I32)
        iota_f = sb("iota_f", [P, SPAN])
        spare_i = sb("spare_i", [P, 1], I32)
        spare_f = sb("spare_f", [P, 1])
        w_type = sb("w_type", [P, TYPES, HID])
        b_type = sb("b_type", [P, HID])
        b_wide = sb("b_wide", [P, TYPES * HID])
        w_ih_rows = sb("w_ih_rows", [P, 3, HID])
        w_hh_rows = sb("w_hh_rows", [P, 3, HID])
        w_ih_T = sb("w_ih_T", [P, GATE])
        w_hh_T = sb("w_hh_T", [P, GATE])
        bi_row = sb("bi_row", [1, GATE])
        bh_row = sb("bh_row", [1, GATE])
        gate_bias = sb("gate_bias", [1, 512])
        bias_rest = sb("bias_rest", [1, 512])
        bias_part = [sb(f"bias_part{n}", [1, 512], BF16) for n in range(PARTS)]
        bias_parts = sb("bias_parts", [P, 512], BF16)
        rows012 = sb("rows012", [P, P], BF16)
        zeros_f = sb("zeros_f", [P, 512])
        idx = sb("idx", [P, ROUND], I32)
        rows = sb("rows", [P, ROUND, HID])
        rest = [sb(f"rest{c}", [P, n, HID]) for c, n in enumerate(GROUPS)]
        parts = [sb(f"parts{c}", [P, n, PARTS, HID], BF16) for c, n in enumerate(GROUPS)]
        node_mask = [sb(f"node_mask{c}", [P, n, SPAN], BF16) for c, n in enumerate(GROUPS)]
        type_mask = [sb(f"type_mask{c}", [P, n, P], BF16) for c, n in enumerate(GROUPS)]
        onehot = [sb(f"onehot{c}", [P, n, SPAN, TYPES], BF16) for c, n in enumerate(GROUPS)]
        sums = sb("sums", [P, TYPES, 3, WINDOW])
        counts = sb("counts", [P, 3, WINDOW])
        messages_T = sb("messages_T", [P, ACC_ROWS])
        x_next = sb("x_next", [P, HID])
        x_tile = sb("x_tile", [P, HID])
        x_T = sb("x_T", [P, P])
        messages = sb("messages", [P, P])
        rz = sb("rz", [P, 2 * HID])
        t_rh = sb("t_rh", [P, HID])
        t_pre = sb("t_pre", [P, HID])
        t_n = sb("t_n", [P, HID])
        t_d = sb("t_d", [P, HID])
        t_zd = sb("t_zd", [P, HID])
        t_h = sb("t_h", [P, HID])
        t_y = sb("t_y", [P, HID])
        stats = sb("stats", [P, nc.vector.BN_STATS_DIM])
        mean_var = sb("mean_var", [P, nc.vector.BN_AGGR_DIM])
        var_eps = sb("var_eps", [P, 1])
        half_bits = sb("half_bits", [P, 1], I32)
        root_a = sb("root_a", [P, 1])
        root_b = sb("root_b", [P, 1])
        rstd = sb("rstd", [P, 1])
        out_tile = sb("out_tile", [P, HID])
        g_dst_T = src_f[:, :, :].rearrange("p b e -> p (b e)")
        g_square = [onehot[c][:, :, :, :].rearrange("p n s t -> p (n s t)").bitcast(F32)[:, k * P:(k + 1) * P]
                    for c in range(2) for k in range(3)]
        g_idx = sb("g_idx", [P, 1], I32)
        g_col = sb("g_col", [P, 1])
        g_wide = g_square[0]
        g_types = sb("g_types", [P, TYPES])
        g_rows = sb("g_rows", [P, HID])
        g_rows_T = g_square[1]
        g_same = g_square[2]
        g_before = g_square[3]
        g_n = sb("g_n", [P, 1])
        g_first = sb("g_first", [P, 1])
        g_rise = sb("g_rise", [P, 1])
        g_row = sb("g_row", [P, 1], I32)
        g_msg = g_square[4]
        g_sum = g_square[5]
        g_acc = sb("g_acc", [P, HID])

        agg = [pb(f"agg{c}") for c in range(3)]
        cnt = [pb(f"cnt{c}") for c in range(2)]
        msg = pb("msg")
        gates = pb("gates")
        xt = pb("xt")

        filled = sem("filled")
        dst_in = sem("dst_in")
        first_in = sem("first_in")
        src_in = sem("src_in")
        type_in = sem("type_in")
        weights_in = sem("weights_in")
        consts = sem("consts")
        zeroed = sem("zeroed")
        prep = sem("prep")
        src0_in = sem("src0_in")
        src0_f_ready = sem("src0_f_ready")
        src0_turned = sem("src0_turned")
        bias_steps = sem("bias_steps")
        bias_split = sem("bias_split")
        bias_in = sem("bias_in")
        banks_zero = sem("banks_zero")
        messages_zero = sem("messages_zero")
        offset_ready = sem("offset_ready")
        rel_ready = sem("rel_ready")
        src_f_ready = sem("src_f_ready")
        type_f_ready = sem("type_f_ready")
        turned = sem("turned")
        turned_copied = sem("turned_copied")
        bad_ready = sem("bad_ready")
        bad_summed = sem("bad_summed")
        fits_ready = sem("fits_ready")
        gathered = [sem(f"gathered{k}") for k in range(ROUND)]
        hi_ready = [sem(f"hi_ready{c}") for c in range(3)]
        rest_ready = [sem(f"rest_ready{c}") for c in range(3)]
        mid_ready = [sem(f"mid_ready{c}") for c in range(3)]
        lo_ready = [sem(f"lo_ready{c}") for c in range(3)]
        idx_ready = [sem(f"idx_ready{c}") for c in range(3)]
        node_mask_ready = [sem(f"node_mask_ready{c}") for c in range(3)]
        type_mask_ready = [sem(f"type_mask_ready{c}") for c in range(3)]
        onehot_ready = [sem(f"onehot_ready{c}") for c in range(3)]
        tiles_done = [sem(f"tiles_done{c}") for c in range(3)]
        sums_read = [sem(f"sums_read{c}") for c in range(3)]
        sums_copied = [sem(f"sums_copied{c}") for c in range(3)]
        applied = sem("applied")
        window_added = [sem(f"window_added{c}") for c in range(2)]
        added = sem("added")
        x_in = sem("x_in")
        x_kept = sem("x_kept")
        xt_ready = sem("xt_ready")
        xt_copied = sem("xt_copied")
        messages_copied = sem("messages_copied")
        gates_ready = sem("gates_ready")
        rz_ready = sem("rz_ready")
        rh_ready = sem("rh_ready")
        pre_ready = sem("pre_ready")
        n_ready = sem("n_ready")
        d_ready = sem("d_ready")
        zd_ready = sem("zd_ready")
        h_ready = sem("h_ready")
        y_ready = sem("y_ready")
        stats_ready = sem("stats_ready")
        mv_ready = sem("mv_ready")
        root_step = [sem(f"root_step{n}") for n in range(3 + 3 * NEWTON)]
        out_ready = sem("out_ready")
        out_stored = sem("out_stored")
        g_dst_f = sem("g_dst_f")
        g_turned = sem("g_turned")
        g_turned_copied = sem("g_turned_copied")
        g_idx_ready = sem("g_idx_ready")
        g_col_ready = sem("g_col_ready")
        g_wide_ready = sem("g_wide_ready")
        g_gathered = sem("g_gathered")
        g_xt_ready = sem("g_xt_ready")
        g_xt_copied = sem("g_xt_copied")
        g_prod_ready = sem("g_prod_ready")
        g_step = sem("g_step")
        g_msg_ready = sem("g_msg_ready")
        g_sum_ready = sem("g_sum_ready")
        g_sum_copied = sem("g_sum_copied")
        g_added = sem("g_added")
        g_acc_in = sem("g_acc_in")
        g_acc_turned = sem("g_acc_turned")
        g_acc_copied = sem("g_acc_copied")

        block = ctx.enter_context(nc.Block())

        TURNS = [(a, b0, min(4, BLOCKS - b0)) for a in range(3) for b0 in range(0, BLOCKS, 4)]
        N_FILLED = 5
        N_CONSTS = 6
        N_ZEROED = 5

        def load_flag(engine):
            engine.wait_ge(fits_ready, 1)
            return nc.values_load(fits[0:1, 0:1], engines=[engine.engine], min_val=0, max_val=1,
                                  skip_runtime_bounds_check_because="it is a product of comparisons")

        def groups_of(last):
            return range(LAST_GROUPS if last else 3)

        def since(r, first):
            return not isinstance(r, int) or r >= first

        def each_round(engine, body):
            for r in range(LAG + 2):
                body(r, False)
            with engine.Fori(LAG + 2, NODE_TILES - 2) as r:
                body(r, False)
            body(NODE_TILES - 2, False)
            body(NODE_TILES - 1, True)

        def each_node_tile(engine, body):
            body(0)
            with engine.Fori(1, NODE_TILES) as j:
                body(j)

        def wait_used(engine, semaphore, count):
            if not (isinstance(count, int) and count == 0):
                engine.wait_ge(semaphore, count)

        @block.sync
        def _(sp):
            def load_rows(tile, values, done):
                whole = (BLOCKS - 1) * P * P
                sp.dma_start(tile[:, 1:BLOCKS - 1, :],
                             values[P * P:whole].rearrange("(b p e) -> p b e", p=P, e=P)).then_inc(done, 16)
                sp.dma_start(tile[0:FULL, BLOCKS - 1, :],
                             values[whole:whole + FULL * P].rearrange("(p e) -> p e", e=P)).then_inc(done, 16)
                sp.dma_start(tile[FULL:FULL + 1, BLOCKS - 1, 0:REST],
                             values[EDGES - REST:EDGES].rearrange("(p e) -> p e", p=1)).then_inc(done, 16)

            sp.dma_start(src_rows[:, 0, :], src[0:P * P].rearrange("(p e) -> p e", e=P)).then_inc(src0_in, 16)
            sp.dma_start(dst_rows[:, 0, :], dst[0:P * P].rearrange("(p e) -> p e", e=P)).then_inc(dst_in, 16)
            sp.wait_ge(filled, N_FILLED)
            load_rows(dst_rows, dst, dst_in)
            load_rows(src_rows, src, src_in)
            sp.dma_start(type_rows[:, 0, :], etype[0:P * P].rearrange("(p e) -> p e", e=P)).then_inc(type_in, 16)
            load_rows(type_rows, etype, type_in)
            sp.wait_ge(zeroed, N_ZEROED)
            sp.dma_start(w_ih_rows[:, :, :], w_ih.rearrange("(a p) h -> p a h", p=P)).then_inc(weights_in, 16)
            sp.dma_start(w_hh_rows[:, :, :], w_hh.rearrange("(a p) h -> p a h", p=P)).then_inc(weights_in, 16)
            sp.dma_start(w_type[:, :, :], w_msg.rearrange("t h d -> h t d")).then_inc(weights_in, 16)
            sp.dma_start(b_type[0:TYPES, :], b_msg).then_inc(weights_in, 16)
            sp.dma_start(b_wide[0:1, :], b_msg.rearrange("(o t) d -> o (t d)", o=1)).then_inc(weights_in, 16)
            sp.dma_start(bi_row[0:1, :], b_ih.rearrange("(o n) -> o n", o=1)).then_inc(weights_in, 16)
            sp.dma_start(bh_row[0:1, :], b_hh.rearrange("(o n) -> o n", o=1)).then_inc(weights_in, 16)
            def load_x(j, n=P):
                wait_used(sp, x_kept, j)
                sp.dma_start(x_next[0:n, :], x[ds(j * P, n), :]).then_inc(x_in, 16)

            def store_out(j, n=P):
                sp.wait_ge(out_ready, j + 1)
                sp.dma_start(out[ds(j * P, n), :], out_tile[0:n, :]).then_inc(out_stored, 16)

            def node_tiles():
                load_x(0)
                sp.wait_ge(bias_split, 1)
                for n in range(PARTS):
                    sp.dma_start(bias_parts[n:n + 1, :], bias_part[n][0:1, :]).then_inc(bias_in, 16)
                with sp.Fori(0, NODE_TILES - 2) as j:
                    load_x(j + 1)
                    store_out(j)
                load_x(NODE_TILES - 1, NODE_LAST)
                store_out(NODE_TILES - 2)
                store_out(NODE_TILES - 1, NODE_LAST)
                sp.wait_ge(out_stored, 16 * NODE_TILES)

            flag = load_flag(sp)
            with sp.If(flag):
                node_tiles()
            with sp.Else():
                sp.wait_ge(g_added, 16 * (TILES + 1))
                def load_acc(j):
                    wait_used(sp, g_acc_copied, j)
                    sp.dma_start(g_acc[:, :], acc[ds(j * P, P), :]).then_inc(g_acc_in, 16)

                each_node_tile(sp, load_acc)
                node_tiles()

        @block.gpsimd
        def _(pool):
            nc.gpsimd.memset(ident[:], 0.0).then_inc(consts, 1)
            nc.gpsimd.memset(ones[:], 1.0).then_inc(consts, 1)
            nc.gpsimd.iota(iota_i[:], pattern=[[1, SPAN]], base=0, channel_multiplier=0).then_inc(consts, 1)
            nc.gpsimd.iota(bound[:], pattern=[[P, NODE_TILES]], base=-P * (LAG - 1),
                           channel_multiplier=0).then_inc(consts, 1)
            nc.gpsimd.iota(spare_i[:], pattern=[[0, 1]], base=NODES, channel_multiplier=1).then_inc(consts, 1)
            pool.wait_ge(consts, 5)
            nc.gpsimd.affine_select(out=ident[:], in_=ident[:], compare_op=ALU.not_equal, fill=1.0, base=0,
                                    pattern=[[-1, P]], channel_multiplier=1)
            nc.gpsimd.affine_select(out=earlier[:], in_=ones[:], compare_op=ALU.is_gt, fill=0.0, base=0,
                                    pattern=[[-1, P]], channel_multiplier=1).then_inc(consts, 1)

            def gather_group(due, c):
                pool.wait_ge(idx_ready[c], due)
                for k in range(START[c], START[c] + GROUPS[c]):
                    nc.gpsimd.indirect_dma_start(
                        out=rows[:, k, :], out_offset=None, in_=x[:, :],
                        in_offset=bass.IndirectOffsetOnAxis(ap=idx[:, k:k + 1], axis=0),
                    ).then_inc(gathered[k], 16)

            nc.gpsimd.memset(messages_T[:, 0:ZERO_A], 0.0).then_inc(messages_zero, 1)
            for c in range(3):
                gather_group(1, c)
            flag = load_flag(pool)
            with pool.If(flag):
                with pool.Fori(2, NODE_TILES) as due:
                    for c in range(3):
                        pool.wait_ge(fits_ready, 1)
                        gather_group(due, c)
                for c in groups_of(last=True):
                    gather_group(NODE_TILES, c)
            with pool.Else():
                pool.wait_ge(messages_zero, N_MESSAGES_ZERO)
                nc.gpsimd.dma_start(acc.rearrange("(p r) d -> p (r d)", p=P), messages_T[:, :]).then_inc(g_added, 16)
                pool.wait_ge(g_added, 16)
                with pool.Fori(1, TILES + 1) as due:
                    pool.wait_ge(fits_ready, 1)
                    pool.wait_ge(g_idx_ready, due)
                    nc.gpsimd.indirect_dma_start(
                        out=g_rows[:, :], out_offset=None, in_=x[:, :],
                        in_offset=bass.IndirectOffsetOnAxis(ap=g_idx[:, 0:1], axis=0),
                    ).then_inc(g_gathered, 16)
                    pool.wait_ge(fits_ready, 1)
                    pool.wait_ge(g_sum_copied, due)
                    nc.gpsimd.indirect_dma_start(
                        out=acc[:, :], out_offset=bass.IndirectOffsetOnAxis(ap=g_row[:, 0:1], axis=0),
                        in_=g_sum[:, :], in_offset=None, compute_op=ALU.add,
                    ).then_inc(g_added, 16)
                    pool.wait_ge(g_added, (due + 1) * 16)

        @block.scalar
        def _(act):
            act.wait_ge(src0_in, 16)
            nc.scalar.activation(src_f[:, 0, :], src_rows[:, 0, :], ACT.Copy).then_inc(src0_f_ready, 1)
            act.wait_ge(src0_turned, 1)
            for c in range(3):
                nc.scalar.activation(idx[:, START[c]:START[c] + GROUPS[c]], xt[:, START[c]:START[c] + GROUPS[c]],
                                     ACT.Copy).then_inc(idx_ready[c], 1)

            with nc.allow_non_contiguous_dma(reason="the first dst of every edge tile, once"):
                act.wait_ge(filled, N_FILLED)
                act.dma_start(first_dst[0:1, 0:TILES],
                              dst[0:EDGES:P].rearrange("(p e) -> p e", p=1)).then_inc(first_in, 16)
                lot = (NODE_TILES - 2) * ROUND * P
                act.dma_start(round_dst[0:NODE_TILES - 2, :],
                              dst[0:lot:P].rearrange("(i k) -> i k", k=ROUND)).then_inc(first_in, 16)
                act.dma_start(round_dst[NODE_TILES - 2:NODE_TILES - 1, :],
                              dst[lot:lot + ROUND * P:P].rearrange("(i k) -> i k", i=1)).then_inc(first_in, 16)
                act.dma_start(round_dst[NODE_TILES - 1:NODE_TILES, 0:LAST],
                              dst[lot + ROUND * P:EDGES:P].rearrange("(i k) -> i k", i=1)).then_inc(first_in, 16)

            act.wait_ge(src_in, 48)
            nc.scalar.activation(src_f[:, 1:BLOCKS, :], src_rows[:, 1:BLOCKS, :], ACT.Copy).then_inc(src_f_ready, 1)
            def next_indices(r, c):
                a = r * ROUND + START[c]
                nc.scalar.activation(idx[:, START[c]:START[c] + GROUPS[c]], src_T[:, ds(a, GROUPS[c])],
                                     ACT.Copy).then_inc(idx_ready[c], 1)

            def hi_part(r, c):
                for k in range(START[c], START[c] + GROUPS[c]):
                    act.wait_ge(gathered[k], (r + 1) * 16)
                wait_used(act, tiles_done[c], r)
                nc.scalar.activation(parts[c][:, :, 0, :], rows[:, START[c]:START[c] + GROUPS[c], :],
                                     ACT.Copy).then_inc(hi_ready[c], 1)

            def mid_part(r, c, more):
                act.wait_ge(rest_ready[c], r + 1)
                nc.scalar.activation(parts[c][:, :, 1, :], rest[c][:, :, :], ACT.Copy).then_inc(mid_ready[c], 1)
                if more:
                    next_indices(r + 1, c)

            def copy_turned(first, last):
                for n in range(first, last):
                    a, b0, nb = TURNS[n]
                    act.wait_ge(turned, n + 1)
                    nc.scalar.activation((src_T, rel_T, type_T)[a][:, b0 * P:(b0 + nb) * P],
                                         agg[n % 3][:, 0:nb * P], ACT.Copy).then_inc(turned_copied, 1)

            per_index = len(TURNS) // 3
            copy_turned(0, per_index)
            act.wait_ge(type_in, 64)
            nc.scalar.activation(type_f[:, :, :], type_rows[:, :, :], ACT.Copy).then_inc(type_f_ready, 1)
            hi_part(0, 0)
            copy_turned(per_index, per_index + 2)
            act.wait_ge(turned_copied, 1)
            mid_part(0, 0, True)
            copy_turned(per_index + 2, len(TURNS))
            hi_part(0, 1)
            act.wait_ge(turned, len(TURNS) + 2)
            nc.scalar.activation(w_ih_T[:, :], gates[:, 0:GATE], ACT.Copy).then_inc(turned_copied, 1)
            nc.scalar.activation(w_hh_T[:, :], msg[:, 0:GATE], ACT.Copy).then_inc(turned_copied, 1)
            mid_part(0, 1, True)
            act.wait_ge(zeroed, 1)
            nc.scalar.activation(messages_T[:, ZERO_A:ZERO_B].rearrange("p (n w) -> p n w", w=P),
                                 zeros_f[:, 0:P].unsqueeze(1).broadcast_to([P, (ZERO_B - ZERO_A) // P, P]),
                                 ACT.Copy).then_inc(messages_zero, 1)

            def zero_banks(c):
                nc.scalar.activation(agg[c][:, :], zeros_f[:, :], ACT.Copy)
                return nc.scalar.activation(cnt[c % 2][:, 0:WINDOW], zeros_f[:, 0:WINDOW], ACT.Copy)

            def copy_sums(r, c):
                act.wait_ge(tiles_done[c], r + 1)
                wait_used(act, applied, r)
                nc.scalar.activation(sums[:, :, c, :],
                                     agg[c][:, :].rearrange("p (n t) -> p t n", t=TYPES), ACT.Copy)
                nc.scalar.activation(counts[:, c, :], cnt[c % 2][:, 0:WINDOW], ACT.Copy).then_inc(sums_read[c], 1)
                act.wait_ge(sums_read[c], r + 1)
                zero_banks(c).then_inc(sums_copied[c], 1)

            def finish_copies(j, nodes_added):
                act.wait_ge(xt_ready, j + 1)
                wait_used(act, gates_ready, j)
                nc.scalar.activation(x_T[:, :], xt[:, 0:P], ACT.Copy).then_inc(xt_copied, 1)
                act.wait_ge(*nodes_added)
                nc.scalar.activation(messages[:, :], messages_T[:, ds(j * P, P)], ACT.Copy).then_inc(messages_copied, 1)

            def keep_x(j):
                wait_used(act, out_ready, j)
                nc.scalar.activation(x_tile[:, :], x_next[:, :], ACT.Copy).then_inc(x_kept, 1)

            def finish_rz(j):
                act.wait_ge(gates_ready, j + 1)
                nc.scalar.activation(rz[:, :], gates[:, 0:2 * HID], ACT.Sigmoid).then_inc(rz_ready, 1)

            def finish_n(j):
                act.wait_ge(pre_ready, j + 1)
                nc.scalar.activation(t_n[:, :], t_pre[:, :], ACT.Tanh).then_inc(n_ready, 1)

            def finish(j, nodes_added):
                finish_copies(j, nodes_added)
                keep_x(j)
                finish_rz(j)
                finish_n(j)

            def round_(r, last):
                def more(c):
                    return not last and (c < LAST_GROUPS or not isinstance(r, int) or r + 1 < NODE_TILES - 1)

                if since(r, 1):
                    hi_part(r, 0)
                    copy_sums(r - 1, 2)
                    mid_part(r, 0, more(0))
                    hi_part(r, 1)
                if since(r, LAG + 1):
                    finish_rz(r - LAG - 1)
                if since(r, 1):
                    mid_part(r, 1, more(1))
                if since(r, LAG + 1):
                    finish_n(r - LAG - 1)
                copy_sums(r, 0)
                if not last:
                    hi_part(r, 2)
                copy_sums(r, 1)
                if since(r, LAG):
                    finish_copies(r - LAG, (added, r))
                if not last:
                    mid_part(r, 2, more(2))
                if since(r, LAG):
                    keep_x(r - LAG)

            flag = load_flag(act)
            with act.If(flag):
                act.wait_ge(turned_copied, len(TURNS))
                zero_banks(0)
                zero_banks(1)
                nc.scalar.activation(agg[2][:, :], zeros_f[:, :], ACT.Copy).then_inc(banks_zero, 1)
                each_round(act, round_)
                finish_rz(NODE_TILES - LAG - 1)
                finish_n(NODE_TILES - LAG - 1)
                for j in range(NODE_TILES - LAG, NODE_TILES):
                    finish(j, (added, NODE_TILES))
            with act.Else():
                for n in range(4):
                    nb = min(4, BLOCKS - 4 * n)
                    act.wait_ge(g_turned, n + 1)
                    nc.scalar.activation(g_dst_T[:, n * 512:n * 512 + nb * P], agg[n % 3][:, 0:nb * P],
                                         ACT.Copy).then_inc(g_turned_copied, 1)
                with act.Fori(0, TILES) as i:
                    act.wait_ge(g_xt_ready, i + 1)
                    nc.scalar.activation(g_rows_T[:, :], agg[0][:, 0:P], ACT.Copy).then_inc(g_xt_copied, 1)
                    act.wait_ge(g_sum_ready, i + 1)
                    nc.scalar.activation(g_sum[:, :], msg[:, 0:HID], ACT.Copy).then_inc(g_sum_copied, 1)
                with act.Fori(0, NODE_TILES) as j:
                    act.wait_ge(g_acc_turned, j + 1)
                    nc.scalar.activation(messages_T[:, ds(j * P, P)], agg[0][:, 0:P], ACT.Copy).then_inc(g_acc_copied, 1)
                each_node_tile(act, lambda j: finish(j, (g_acc_copied, NODE_TILES)))

        @block.vector
        def _(dve):
            steps = [0]

            def step(ins):
                steps[0] += 1
                ins.then_inc(prep, 1)
                dve.wait_ge(prep, steps[0])

            nc.vector.memset(zeros_f[:], 0.0).then_inc(zeroed, 1)
            nc.vector.memset(dst_rows[:, BLOCKS - 1, :], PAD_ROW).then_inc(filled, 1)
            nc.vector.memset(first_dst[0:1, TILES:ROW], PAD_ROW).then_inc(filled, 1)
            nc.vector.memset(round_dst[:, :], PAD_ROW).then_inc(filled, 1)
            nc.vector.memset(src_rows[:, BLOCKS - 1, :], 0).then_inc(filled, 1)
            nc.vector.memset(type_rows[:, BLOCKS - 1, :], 0).then_inc(filled, 1)
            nc.vector.memset(b_type[:], 0.0)
            nc.vector.memset(b_wide[:], 0.0)
            nc.vector.memset(bias_parts[:], 0.0).then_inc(zeroed, 1)
            for c in range(3):
                last = nc.vector.memset(type_mask[c][:], 0.0)
            last.then_inc(zeroed, 1)
            step(nc.vector.memset(row0[:], 0.0))
            nc.vector.memset(row0[0:1, :], 1.0).then_inc(zeroed, 1)
            step(nc.vector.memset(rows012[:], 0.0))
            nc.vector.memset(rows012[0:PARTS, :], 1.0).then_inc(zeroed, 1)
            step(nc.vector.memset(extremes[:], 0.0))
            nc.vector.memset(messages_T[:, ZERO_B:ACC_ROWS], 0.0).then_inc(messages_zero, 1)

            def check_spans():
                dve.wait_ge(dst_in, 64)
                nc.vector.tensor_tensor(rel_f[:, :, :], dst_rows[:, :, :],
                                        dst_rows[:, :, 0:1].broadcast_to([P, BLOCKS, P]), ALU.subtract).then_inc(rel_ready, 1)
                dve.wait_ge(rel_ready, 1)
                b = BLOCKS - 1
                for a, op in enumerate((ALU.max, ALU.min)):
                    nc.vector.tensor_reduce(extremes[:, 3 * a:3 * a + 1],
                                            rel_f[:, 0:b, :].rearrange("p b e -> p (b e)"), AX, op)
                    nc.vector.tensor_reduce(extremes[0:FULL + 1, 3 * a + 1:3 * a + 2], rel_f[0:FULL + 1, b, 0:REST], AX, op)
                    last = nc.vector.tensor_reduce(extremes[0:FULL, 3 * a + 2:3 * a + 3], rel_f[0:FULL, b, REST:P], AX, op)
                step(last)
                nc.vector.tensor_scalar(bad[:, 0:3], extremes[:, 0:3], float(SPAN - 1), None, ALU.is_gt)
                nc.vector.tensor_scalar(bad[:, 3:6], extremes[:, 3:6], 0.0, None, ALU.is_lt)

            def check_tiles():
                dve.wait_ge(first_in, 4 * 16)
                dve.wait_ge(consts, N_CONSTS)
                first = first_dst[0:1, :].rearrange("p (i k) -> p i k", k=ROUND)
                for c, n in enumerate(GROUPS):
                    a = START[c]
                    nc.vector.tensor_tensor(round_off[:, a:a + n], round_dst[:, a:a + n],
                                            round_dst[:, a:a + 1].broadcast_to([NODE_TILES, n]), ALU.subtract)
                nc.vector.tensor_tensor(round_rise[:, 0:ROUND - 1], round_dst[:, 1:ROUND], round_dst[:, 0:ROUND - 1], ALU.subtract)
                nc.vector.tensor_tensor(seam[0:1, 0:NODE_TILES - 1], first[:, 1:NODE_TILES, 0],
                                        first[:, 0:NODE_TILES - 1, ROUND - 1], ALU.subtract)
                step(nc.vector.tensor_tensor(ahead[0:1, :], first[:, :, 0], bound[0:1, :], ALU.subtract))
                nc.vector.tensor_reduce(extremes[0:NODE_TILES, 6:7], round_off[:, :], AX, ALU.max)
                nc.vector.tensor_reduce(extremes[0:NODE_TILES, 7:8], round_rise[:, 0:ROUND - 1], AX, ALU.min)
                nc.vector.tensor_reduce(extremes[0:1, 8:9], seam[0:1, 0:NODE_TILES - 1], AX, ALU.min)
                step(nc.vector.tensor_reduce(extremes[0:1, 9:10], ahead[0:1, :], AX, ALU.min))
                nc.vector.tensor_scalar(bad[:, 6:7], extremes[:, 6:7], float(WINDOW - SPAN), None, ALU.is_gt)
                nc.vector.tensor_scalar(bad[:, 7:10], extremes[:, 7:10], 0.0, None, ALU.is_lt).then_inc(bad_ready, 1)

            def decide():
                dve.wait_ge(bad_summed, 1)
                step(nc.vector.tensor_reduce(bad_sum[0:1, 0:1], cnt[0][0:1, 0:10], AX, ALU.add))
                nc.vector.tensor_scalar(fits[0:1, 0:1], bad_sum[0:1, 0:1], 0.5, None, ALU.is_lt).then_inc(fits_ready, 1)

            def make_offsets():
                first = first_dst[0:1, :].rearrange("p (i k) -> p i k", k=ROUND)
                off = offset[0:1, :].rearrange("p (i k) -> p i k", k=ROUND)
                for a, n in zip(START, GROUPS):
                    last = nc.vector.tensor_tensor(off[:, :, a:a + n], first[:, :, a:a + n],
                                                   first[:, :, a:a + 1].broadcast_to([1, NODE_TILES, n]), ALU.subtract)
                last.then_inc(offset_ready, 1)

            def split_bias():
                done = [0]

                def bias_step(ins):
                    done[0] += 1
                    ins.then_inc(bias_steps, 1)
                    dve.wait_ge(bias_steps, done[0])

                dve.wait_ge(weights_in, 7 * 16)
                nc.vector.tensor_tensor(gate_bias[0:1, 0:2 * HID], bi_row[0:1, 0:2 * HID], bh_row[0:1, 0:2 * HID], ALU.add)
                nc.vector.tensor_copy(gate_bias[0:1, 2 * HID:3 * HID], bi_row[0:1, 2 * HID:GATE])
                bias_step(nc.vector.tensor_copy(gate_bias[0:1, 3 * HID:4 * HID], bh_row[0:1, 2 * HID:GATE]))
                bias_step(nc.vector.tensor_copy(bias_part[0][0:1, :], gate_bias[0:1, :]))
                bias_step(nc.vector.tensor_tensor(bias_rest[0:1, :], gate_bias[0:1, :], bias_part[0][0:1, :], ALU.subtract))
                bias_step(nc.vector.tensor_copy(bias_part[1][0:1, :], bias_rest[0:1, :]))
                nc.vector.tensor_tensor(bias_part[2][0:1, :], bias_rest[0:1, :], bias_part[1][0:1, :],
                                        ALU.subtract).then_inc(bias_split, 1)

            def rest_part(r, c):
                dve.wait_ge(hi_ready[c], r + 1)
                wait_used(dve, lo_ready[c], r)
                nc.vector.tensor_tensor(rest[c][:, :, :], rows[:, START[c]:START[c] + GROUPS[c], :],
                                        parts[c][:, :, 0, :], ALU.subtract).then_inc(rest_ready[c], 1)

            def lo_part(r, c):
                dve.wait_ge(mid_ready[c], r + 1)
                nc.vector.tensor_tensor(parts[c][:, :, 2, :], rest[c][:, :, :],
                                        parts[c][:, :, 1, :], ALU.subtract).then_inc(lo_ready[c], 1)

            check_spans()
            check_tiles()
            decide()
            rest_part(0, 0)
            make_offsets()
            nc.vector.tensor_copy(iota_f[:, :], iota_i[:, :])
            step(nc.vector.tensor_copy(spare_f[:, :], spare_i[:, :]))
            lo_part(0, 0)
            rest_part(0, 1)
            lo_part(0, 1)

            def masks(r, c):
                n, a = GROUPS[c], r * ROUND + START[c]
                wait_used(dve, tiles_done[c], r)
                nc.vector.tensor_tensor(
                    node_mask[c][:, :, :], rel_T[:, ds(a, n)].unsqueeze(2).broadcast_to([P, n, SPAN]),
                    iota_f[:, :].unsqueeze(1).broadcast_to([P, n, SPAN]), ALU.is_equal).then_inc(node_mask_ready[c], 1)
                nc.vector.tensor_tensor(
                    type_mask[c][:, :, 0:TYPES], type_T[:, ds(a, n)].unsqueeze(2).broadcast_to([P, n, TYPES]),
                    iota_f[:, 0:TYPES].unsqueeze(1).broadcast_to([P, n, TYPES]),
                    ALU.is_equal).then_inc(type_mask_ready[c], 1)
                dve.wait_ge(node_mask_ready[c], r + 1)
                dve.wait_ge(type_mask_ready[c], r + 1)
                nc.vector.tensor_tensor(
                    onehot[c][:, :, :, :], node_mask[c][:, :, :].unsqueeze(3).broadcast_to([P, n, SPAN, TYPES]),
                    type_mask[c][:, :, 0:TYPES].unsqueeze(2).broadcast_to([P, n, SPAN, TYPES]),
                    ALU.mult).then_inc(onehot_ready[c], 1)

            def add_messages(r, groups=3):
                nodes = [nc.values_load(first_dst[0:1, ds(r * ROUND + START[c], 1)], engines=[dve.engine],
                                        min_val=0, max_val=NODES - 1,
                                        skip_runtime_bounds_check_because="a dst of a real edge")
                         for c in range(groups)]
                dve.wait_ge(applied, r + 1)
                for c, node in enumerate(nodes):
                    ins = nc.vector.tensor_tensor(messages_T[:, ds(node, WINDOW)], messages_T[:, ds(node, WINDOW)],
                                                  msg[:, c * WINDOW:(c + 1) * WINDOW], ALU.add)
                    if c < groups - 1:
                        ins.then_inc(window_added[c], 1)
                        dve.wait_ge(window_added[c], r + 1)
                ins.then_inc(added, 1)

            def inverse_root(j):
                nc.vector.tensor_scalar(var_eps[:, :], mean_var[:, 1:2], EPS, None, ALU.add).then_inc(root_step[0], 1)
                dve.wait_ge(root_step[0], j + 1)
                nc.vector.tensor_scalar(half_bits[:, :], var_eps[:, :].bitcast(I32), 1, None,
                                        ALU.logical_shift_right).then_inc(root_step[1], 1)
                dve.wait_ge(root_step[1], j + 1)
                nc.vector.tensor_scalar(rstd[:, :].bitcast(I32), half_bits[:, :], -1.0, float(0x5F3759DF),
                                        ALU.mult, ALU.add).then_inc(root_step[2], 1)
                dve.wait_ge(root_step[2], j + 1)
                for n in range(NEWTON):
                    nc.vector.scalar_tensor_tensor(out=root_a[:, :], in0=rstd[:, :], scalar=rstd[:, 0:1], in1=var_eps[:, :],
                                                   op0=ALU.mult, op1=ALU.mult).then_inc(root_step[3 + 3 * n], 1)
                    dve.wait_ge(root_step[3 + 3 * n], j + 1)
                    nc.vector.tensor_scalar(root_b[:, :], root_a[:, :], -0.5, 1.5, ALU.mult, ALU.add).then_inc(root_step[4 + 3 * n], 1)
                    dve.wait_ge(root_step[4 + 3 * n], j + 1)
                    nc.vector.tensor_tensor(rstd[:, :], rstd[:, :], root_b[:, :], ALU.mult).then_inc(root_step[5 + 3 * n], 1)
                    dve.wait_ge(root_step[5 + 3 * n], j + 1)

            def finish_pre(j):
                dve.wait_ge(rz_ready, j + 1)
                nc.vector.tensor_tensor(t_rh[:, :], rz[:, 0:HID], gates[:, 3 * HID:4 * HID], ALU.mult).then_inc(rh_ready, 1)
                dve.wait_ge(rh_ready, j + 1)
                nc.vector.tensor_tensor(t_pre[:, :], t_rh[:, :], gates[:, 2 * HID:3 * HID], ALU.add).then_inc(pre_ready, 1)

            def finish_out(j):
                dve.wait_ge(n_ready, j + 1)
                nc.vector.tensor_tensor(t_d[:, :], x_tile[:, :], t_n[:, :], ALU.subtract).then_inc(d_ready, 1)
                dve.wait_ge(d_ready, j + 1)
                nc.vector.tensor_tensor(t_zd[:, :], t_d[:, :], rz[:, HID:2 * HID], ALU.mult).then_inc(zd_ready, 1)
                dve.wait_ge(zd_ready, j + 1)
                nc.vector.tensor_tensor(t_h[:, :], t_zd[:, :], t_n[:, :], ALU.add).then_inc(h_ready, 1)
                dve.wait_ge(h_ready, j + 1)
                nc.vector.tensor_tensor(t_y[:, :], t_h[:, :], x_tile[:, :], ALU.add).then_inc(y_ready, 1)
                dve.wait_ge(y_ready, j + 1)
                nc.vector.bn_stats(stats[:, :], t_y[:, :]).then_inc(stats_ready, 1)
                dve.wait_ge(fits_ready, 1)
                dve.wait_ge(stats_ready, j + 1)
                nc.vector.bn_aggr(mean_var[:, :], stats[:, :]).then_inc(mv_ready, 1)
                dve.wait_ge(mv_ready, j + 1)
                inverse_root(j)
                wait_used(dve, out_stored, j * 16)
                nc.vector.tensor_scalar(out_tile[:, :], t_y[:, :], mean_var[:, 0:1], rstd[:, 0:1],
                                        ALU.subtract, ALU.mult).then_inc(out_ready, 1)

            def finish(j):
                finish_pre(j)
                finish_out(j)

            def round_(r, last):
                if since(r, 1):
                    rest_part(r, 0)
                    masks(r, 1)
                    lo_part(r, 0)
                    rest_part(r, 1)
                if since(r, LAG + 1):
                    finish_pre(r - LAG - 1)
                if since(r, 1) and not last:
                    masks(r, 2)
                if since(r, 1):
                    lo_part(r, 1)
                if since(r, 1):
                    add_messages(r - 1)
                if since(r, LAG + 1):
                    finish_out(r - LAG - 1)
                if not last:
                    rest_part(r, 2)
                    masks(r + 1, 0)
                    lo_part(r, 2)
                if not since(r, 1):
                    split_bias()

            flag = load_flag(dve)
            with dve.If(flag):
                dve.wait_ge(turned_copied, len(TURNS))
                for c in range(3):
                    masks(0, c)
                dve.wait_ge(messages_zero, N_MESSAGES_ZERO)
                each_round(dve, round_)
                add_messages(NODE_TILES - 1, LAST_GROUPS)
                finish_pre(NODE_TILES - LAG - 1)
                finish_out(NODE_TILES - LAG - 1)
                for j in range(NODE_TILES - LAG, NODE_TILES):
                    finish(j)
            with dve.Else():
                dve.wait_ge(turned_copied, len(TURNS))
                nc.vector.tensor_copy(rel_f[:, :, :], dst_rows[:, :, :]).then_inc(g_dst_f, 1)
                split_bias()
                dve.wait_ge(g_turned_copied, 4)
                STEPS = 6 + TYPES
                with dve.Fori(0, TILES) as i:
                    done = [0]

                    def g(ins):
                        done[0] += 1
                        ins.then_inc(g_step, 1)
                        dve.wait_ge(g_step, i * STEPS + done[0])

                    dve.wait_ge(g_added, (i + 1) * 16)
                    nc.vector.tensor_copy(g_idx[:, :], src_T[:, ds(i, 1)]).then_inc(g_idx_ready, 1)
                    g(nc.vector.tensor_copy(g_col[:, :], g_dst_T[:, ds(i, 1)]))
                    nc.vector.tensor_copy(g_wide[:, :], g_col[:, 0:1].broadcast_to([P, P])).then_inc(g_wide_ready, 1)
                    g(nc.vector.tensor_tensor(g_types[:, :], type_T[:, ds(i, 1)].broadcast_to([P, TYPES]),
                                              iota_f[:, 0:TYPES], ALU.is_equal))
                    dve.wait_ge(g_xt_ready, i + 1)
                    g(nc.vector.tensor_scalar(g_same[:, :], agg[1][:, 0:P], g_col[:, 0:1], None, ALU.is_equal))
                    g(nc.vector.tensor_tensor(g_before[:, :], g_same[:, :], earlier[:, :], ALU.mult))
                    g(nc.vector.tensor_reduce(g_n[:, :], g_before[:, :], AX, ALU.add))
                    nc.vector.tensor_scalar(g_first[:, :], g_n[:, :], 0.5, None, ALU.is_lt)
                    g(nc.vector.tensor_tensor(g_rise[:, :], g_col[:, :], spare_f[:, :], ALU.subtract))
                    nc.vector.scalar_tensor_tensor(out=g_row[:, :], in0=g_rise[:, :], scalar=g_first[:, 0:1],
                                                   in1=spare_f[:, :], op0=ALU.mult, op1=ALU.add)
                    dve.wait_ge(g_prod_ready, i + 1)
                    g(nc.vector.tensor_scalar(g_msg[:, :], agg[2][:, 0:HID], g_types[:, 0:1], None, ALU.mult))
                    for t in range(1, TYPES):
                        bank = agg[2] if t < 4 else cnt[0]
                        ins = nc.vector.scalar_tensor_tensor(
                            out=g_msg[:, :], in0=bank[:, t % 4 * HID:(t % 4 + 1) * HID], scalar=g_types[:, t:t + 1],
                            in1=g_msg[:, :], op0=ALU.mult, op1=ALU.add)
                        if t < TYPES - 1:
                            g(ins)
                    ins.then_inc(g_step, 1)
                    assert done[0] + 1 == STEPS
                    dve.wait_ge(g_step, (i + 1) * STEPS)
                    nc.vector.tensor_copy(g_types[:, 0:1], g_n[:, 0:1]).then_inc(g_msg_ready, 1)
                each_node_tile(dve, finish)

        @block.tensor
        def _(pe):
            pe.wait_ge(consts, N_CONSTS)
            pe.wait_ge(src0_f_ready, 1)
            nc.tensor.transpose(xt[:, 0:P], src_f[:, 0, :], ident[:, :]).then_inc(src0_turned, 1)
            for n, (a, b0, nb) in enumerate(TURNS):
                if n >= 3:
                    pe.wait_ge(turned_copied, n - 2)
                pe.wait_ge((src_f_ready, rel_ready, type_f_ready)[a], 1)
                for b in range(nb):
                    last = nc.tensor.transpose(agg[n % 3][:, b * P:(b + 1) * P],
                                               (src_f, rel_f, type_f)[a][:, b0 + b, :], ident[:, :])
                last.then_inc(turned, 1)
                if n == 3:
                    pe.wait_ge(bad_ready, 1)
                    nc.tensor.matmul(cnt[0][:, 0:10], ones[:, :], bad[:, :], start=True, stop=True).then_inc(bad_summed, 1)
            pe.wait_ge(weights_in, 7 * 16)
            for bank, w in ((gates, w_ih_rows), (msg, w_hh_rows)):
                for a in range(3):
                    last = nc.tensor.transpose(bank[:, a * P:(a + 1) * P], w[:, a, :], ident[:, :])
                last.then_inc(turned, 1)
            pe.wait_ge(turned_copied, len(TURNS) + 2)
            pe.wait_ge(zeroed, N_ZEROED)
            pe.wait_ge(offset_ready, 1)

            def sum_tiles(r, c):
                n, a = GROUPS[c], r * ROUND + START[c]
                counts_bank = cnt[c % 2]
                _, offs = nc.values_load_multi_w_load_instructions(
                    offset[0:1, ds(a, n)], engines=[pe.engine], min_val=0, max_val=WINDOW - SPAN,
                    skip_runtime_bounds_check_because="checked on the chip before this path is taken")
                if isinstance(r, int) and r == 0:
                    pe.wait_ge(banks_zero, 1)
                else:
                    pe.wait_ge(sums_copied[c], r)
                    if c == 0:
                        pe.wait_ge(sums_copied[2], r)
                if c == 2:
                    pe.wait_ge(sums_copied[0], r + 1)
                pe.wait_ge(onehot_ready[c], r + 1)
                pe.wait_ge(lo_ready[c], r + 1)
                for k in range(n):
                    nc.tensor.matmul(counts_bank[:, ds(offs[k], SPAN)], type_mask[c][:, k, :], node_mask[c][:, k, :],
                                     start=False, stop=True, skip_group_check=True)
                    for part in range(PARTS):
                        last = nc.tensor.matmul(agg[c][:, ds(offs[k] * TYPES, SPAN * TYPES)],
                                                parts[c][:, k, part, :],
                                                onehot[c][:, k, :, :].rearrange("p n t -> p (n t)"),
                                                start=False, stop=True, skip_group_check=True)
                last.then_inc(tiles_done[c], 1)

            def apply_weights(r, groups=3):
                pe.wait_ge(sums_copied[groups - 1], r + 1)
                wait_used(pe, added, r)
                out_cols = msg[:, 0:groups * WINDOW]
                nc.tensor.matmul(out_cols, b_type[:, :], counts[:, 0:groups, :].rearrange("p c n -> p (c n)"),
                                 start=True, stop=False)
                for t in range(TYPES):
                    last = nc.tensor.matmul(out_cols, w_type[:, t, :], sums[:, t, 0:groups, :].rearrange("p c n -> p (c n)"),
                                            start=False, stop=t == TYPES - 1)
                last.then_inc(applied, 1)

            def turn_x(j):
                pe.wait_ge(x_in, (j + 1) * 16)
                wait_used(pe, xt_copied, j)
                nc.tensor.transpose(xt[:, 0:P], x_next[:, :], ident[:, :]).then_inc(xt_ready, 1)

            def make_gates(j):
                wait_used(pe, pre_ready, j)
                if isinstance(j, int) and j == 0:
                    pe.wait_ge(bias_in, PARTS * 16)
                nc.tensor.matmul(gates[:, :], rows012[:, :], bias_parts[:, :], start=True, stop=False)
                pe.wait_ge(xt_copied, j + 1)
                nc.tensor.matmul(gates[:, 0:2 * HID], x_T[:, :], w_hh_T[:, 0:2 * HID], start=False, stop=False)
                nc.tensor.matmul(gates[:, 3 * HID:4 * HID], x_T[:, :], w_hh_T[:, 2 * HID:GATE], start=False, stop=False)
                pe.wait_ge(messages_copied, j + 1)
                nc.tensor.matmul(gates[:, 0:GATE], messages[:, :], w_ih_T[:, :], start=False, stop=True).then_inc(gates_ready, 1)

            def finish(j):
                turn_x(j)
                make_gates(j)

            def round_(r, last):
                if since(r, 1):
                    apply_weights(r - 1)
                if since(r, LAG):
                    turn_x(r - LAG)
                sum_tiles(r, 0)
                sum_tiles(r, 1)
                if not last:
                    sum_tiles(r, 2)
                if since(r, LAG):
                    make_gates(r - LAG)

            flag = load_flag(pe)
            with pe.If(flag):
                each_round(pe, round_)
                apply_weights(NODE_TILES - 1, LAST_GROUPS)
                for j in range(NODE_TILES - LAG, NODE_TILES):
                    finish(j)
            with pe.Else():
                pe.wait_ge(g_dst_f, 1)
                for n in range(4):
                    if n == 3:
                        pe.wait_ge(g_turned_copied, 1)
                    for b in range(4 * n, min(4 * n + 4, BLOCKS)):
                        last = nc.tensor.transpose(agg[n % 3][:, (b % 4) * P:(b % 4 + 1) * P], rel_f[:, b, :], ident[:, :])
                    last.then_inc(g_turned, 1)
                pe.wait_ge(g_turned_copied, 4)
                with pe.Fori(0, TILES) as i:
                    pe.wait_ge(g_wide_ready, i + 1)
                    nc.tensor.transpose(agg[1][:, 0:P], g_wide[:, :], ident[:, :])
                    pe.wait_ge(g_gathered, (i + 1) * 16)
                    nc.tensor.transpose(agg[0][:, 0:P], g_rows[:, :], ident[:, :]).then_inc(g_xt_ready, 1)
                    pe.wait_ge(g_xt_copied, i + 1)
                    for h, bank in enumerate((agg[2], cnt[0])):
                        cols = slice(h * 4 * HID, (h + 1) * 4 * HID)
                        nc.tensor.matmul(bank[:, :], row0[:, :], b_wide[:, cols], start=True, stop=False)
                        last = nc.tensor.matmul(bank[:, :], g_rows_T[:, :],
                                                w_type[:, 4 * h:4 * h + 4, :].rearrange("p t d -> p (t d)"),
                                                start=False, stop=True)
                    last.then_inc(g_prod_ready, 1)
                    pe.wait_ge(g_msg_ready, i + 1)
                    nc.tensor.matmul(msg[:, 0:HID], g_same[:, :], g_msg[:, :], start=True, stop=True).then_inc(g_sum_ready, 1)
                def turn_acc(j):
                    pe.wait_ge(g_acc_in, (j + 1) * 16)
                    wait_used(pe, g_acc_copied, j)
                    nc.tensor.transpose(agg[0][:, 0:P], g_acc[:, :], ident[:, :]).then_inc(g_acc_turned, 1)

                each_node_tile(pe, turn_acc)
                pe.wait_ge(g_acc_copied, NODE_TILES)
                each_node_tile(pe, finish)


_INS = ['x', 'src', 'dst', 'edge_type_8', 'L0_gnn_message_W', 'L0_gnn_message_b', 'L0_gnn_gru_w_ih',
        'L0_gnn_gru_w_hh', 'L0_gnn_gru_b_ih', 'L0_gnn_gru_b_hh']


def kernel(**inputs):
    import numpy as _np
    import concourse.bacc as _bacc
    from concourse import mybir as _mybir
    from concourse.bass_utils import run_bass_kernel_spmd as _run

    nc = _bacc.Bacc("TRN2", target_bir_lowering=False, num_devices=1)
    arrays, args = {}, []
    for name in _INS:
        a = _np.ascontiguousarray(inputs[name])
        arrays[f"in_{name}_dram"] = a
        args.append(nc.dram_tensor(f"in_{name}_dram", a.shape, _mybir.dt.from_np(a.dtype), kind="ExternalInput").ap())
    args.append(nc.dram_tensor("out_dram", arrays["in_x_dram"].shape, _mybir.dt.float32, kind="ExternalOutput").ap())
    gnn_kernel(nc, *args)
    r = _run(nc, [arrays], core_ids=[0])
    return r.results[0]["out_dram"]
```
